# Optimizing a Trainium2 kernel written in Bass

```python
import numpy as np
import jax
import jax.numpy as jnp

def _softmax(x, axis=-1):
    return jax.nn.softmax(x, axis=axis)

def _gelu(x):
    return jax.nn.gelu(x, approximate=True)

def _silu(x):
    return jax.nn.silu(x)

def _sigmoid(x):
    return jax.nn.sigmoid(x)

def _layernorm(x, axis=-1, eps=1e-05):
    m = jnp.mean(x, axis=axis, keepdims=True)
    v = jnp.var(x, axis=axis, keepdims=True)
    return (x - m) / jnp.sqrt(v + eps)

def _scatter_add(tgt, idx, src, axis=0):
    return tgt.at[idx].add(src)

def _segment_sum(src, seg, n):
    return jax.ops.segment_sum(src, seg, n)
kernel_name = 'mk_xattn_ffn_d1_seqx_r2_a4f768'

def setup_inputs(seed: int=0):
    np.random.seed(seed)
    _w = jnp.asarray

    def _rec_inputs():
        import jax
        import jax.numpy as jnp
        _rk = jax.random.key(seed)
        x = 7.22e-05 + 1 * jax.random.normal(jax.random.fold_in(_rk, 1), (2, 2048, 512), jnp.float32)
        _lenS = 2048 - jax.random.randint(jax.random.fold_in(_rk, 7), (2,), 0, max(1, 2048 // 4) + 1, jnp.int32)
        _lenS2 = 77 - jax.random.randint(jax.random.fold_in(_rk, 8), (2,), 0, max(1, 77 // 4) + 1, jnp.int32)
        _ctx_1024P = jax.random.normal(jax.random.fold_in(_rk, 11), (2, 16, 512), jnp.float32)
        _ctx_1024c = jax.random.dirichlet(jax.random.fold_in(_rk, 511), 0.3 * jnp.ones((16,), jnp.float32), (2, 77))
        _ctx_1024t = jnp.einsum('bsk,bkd->bsd', _ctx_1024c, _ctx_1024P)
        _ctx_1024t = _ctx_1024t * jax.lax.rsqrt(jnp.mean(jnp.square(_ctx_1024t)) + 1e-12) * 0.953939
        ctx_1024 = 4.13588e-05 + 0.999923 * (_ctx_1024t + 0.3 * jax.random.normal(jax.random.fold_in(_rk, 611), (2, 77, 512), jnp.float32))
        _validS = jnp.arange(2048)[None, :] < _lenS[:, None]
        _validS2 = jnp.arange(77)[None, :] < _lenS2[:, None]
        _causal = jnp.tril(jnp.ones((2048, 2048), dtype=bool))
        mask_SxS2_bk1 = jnp.broadcast_to(_validS2[0:1, :], (2048, 77))
        return (x, ctx_1024, mask_SxS2_bk1)
    x, ctx_1024, mask_SxS2_bk1 = _rec_inputs()

    def _L0_xattn_setup():
        import math
        import jax, jax.numpy as jnp
        import numpy as np
        EMBED_DIM = 512
        NUM_HEADS = 16
        HEAD_DIM = EMBED_DIM // NUM_HEADS
        B, S = (4, 1024)

        def _split_heads(x):
            b, s, _ = x.shape
            return x.reshape(b, s, NUM_HEADS, HEAD_DIM).transpose(0, 2, 1, 3)
        key = jax.random.key(seed)
        ks = jax.random.split(key, 12)
        sc = 1.0 / math.sqrt(EMBED_DIM)
        inp = {'query': jax.random.normal(ks[0], (B, S, EMBED_DIM), jnp.float32), 'key': jax.random.normal(ks[1], (B, S, EMBED_DIM), jnp.float32), 'value': jax.random.normal(ks[2], (B, S, EMBED_DIM), jnp.float32), 'attn_mask': jnp.triu(jnp.ones((S, S), jnp.bool_), k=1), 'q_w': jax.random.normal(ks[3], (EMBED_DIM, EMBED_DIM), jnp.float32) * sc, 'q_b': jax.random.normal(ks[4], (EMBED_DIM,), jnp.float32) * sc, 'k_w': jax.random.normal(ks[5], (EMBED_DIM, EMBED_DIM), jnp.float32) * sc, 'k_b': jax.random.normal(ks[6], (EMBED_DIM,), jnp.float32) * sc, 'v_w': jax.random.normal(ks[7], (EMBED_DIM, EMBED_DIM), jnp.float32) * sc, 'v_b': jax.random.normal(ks[8], (EMBED_DIM,), jnp.float32) * sc, 'o_w': jax.random.normal(ks[9], (EMBED_DIM, EMBED_DIM), jnp.float32) * sc, 'o_b': jax.random.normal(ks[10], (EMBED_DIM,), jnp.float32) * sc}
        return inp
    _L0_xattn_all = _L0_xattn_setup()
    _L0_xattn_in = {k: v for k, v in _L0_xattn_all.items() if k in ('q_w', 'q_b', 'k_w', 'k_b', 'v_w', 'v_b', 'o_w', 'o_b')}
    del _L0_xattn_all

    def _L0_ffn_setup():
        import jax, jax.numpy as jnp
        import numpy as np
        EPS = 1e-09
        key = jax.random.key(seed)
        k1, k2, k3, k4 = jax.random.split(key, 4)
        B, T, H, D, E = (2, 1024, 512, 512, 8)
        x = jax.random.normal(k1, (B, T, H), dtype=jnp.float32)
        gate_w = jax.random.normal(k2, (E, H), dtype=jnp.float32) * 0.02
        gate_up_proj = jax.random.normal(k3, (E, H, 2 * D), dtype=jnp.float32) * 0.02
        down_proj = jax.random.normal(k4, (E, D, H), dtype=jnp.float32) * 0.02
        return {'x': x, 'gate_w': gate_w, 'gate_up_proj': gate_up_proj, 'down_proj': down_proj}
    _L0_ffn_all = _L0_ffn_setup()
    _L0_ffn_in = {k: v for k, v in _L0_ffn_all.items() if k in ('gate_w', 'gate_up_proj', 'down_proj')}
    del _L0_ffn_all
    return {'x': x, 'ctx_1024': ctx_1024, 'mask_SxS2_bk1': mask_SxS2_bk1, 'L0_xattn_q_w': _L0_xattn_in['q_w'], 'L0_xattn_q_b': _L0_xattn_in['q_b'], 'L0_xattn_k_w': _L0_xattn_in['k_w'], 'L0_xattn_k_b': _L0_xattn_in['k_b'], 'L0_xattn_v_w': _L0_xattn_in['v_w'], 'L0_xattn_v_b': _L0_xattn_in['v_b'], 'L0_xattn_o_w': _L0_xattn_in['o_w'], 'L0_xattn_o_b': _L0_xattn_in['o_b'], 'L0_ffn_gate_w': _L0_ffn_in['gate_w'], 'L0_ffn_gate_up_proj': _L0_ffn_in['gate_up_proj'], 'L0_ffn_down_proj': _L0_ffn_in['down_proj']}

def reference(x, ctx_1024, mask_SxS2_bk1, L0_xattn_q_w, L0_xattn_q_b, L0_xattn_k_w, L0_xattn_k_b, L0_xattn_v_w, L0_xattn_v_b, L0_xattn_o_w, L0_xattn_o_b, L0_ffn_gate_w, L0_ffn_gate_up_proj, L0_ffn_down_proj):
    import jax
    import jax.numpy as jnp

    def _L0_xattn_ref(query, key, value, attn_mask, q_w, q_b, k_w, k_b, v_w, v_b, o_w, o_b):
        import math
        import jax, jax.numpy as jnp
        import numpy as np
        EMBED_DIM = 512
        NUM_HEADS = 16
        HEAD_DIM = EMBED_DIM // NUM_HEADS
        B, S = (4, 1024)

        def _split_heads(x):
            b, s, _ = x.shape
            return x.reshape(b, s, NUM_HEADS, HEAD_DIM).transpose(0, 2, 1, 3)
        q = _split_heads(query @ q_w.T + q_b)
        k = _split_heads(key @ k_w.T + k_b)
        v = _split_heads(value @ v_w.T + v_b)
        scale = math.sqrt(HEAD_DIM)
        scores = jnp.einsum('bhqd,bhkd->bhqk', q, k) / scale
        scores = jnp.where(attn_mask[None, None, :, :], -jnp.inf, scores)
        attn = jax.nn.softmax(scores, axis=-1)
        ctx = jnp.einsum('bhqk,bhkd->bhqd', attn, v)
        ctx = ctx.transpose(0, 2, 1, 3).reshape(query.shape[0], query.shape[1], EMBED_DIM)
        return ctx @ o_w.T + o_b

    def _L0_ffn_ref(x, gate_w, gate_up_proj, down_proj):
        import jax, jax.numpy as jnp
        import numpy as np
        EPS = 1e-09
        B, T, H = x.shape
        E = gate_w.shape[0]
        top_k = 2
        hidden = x.reshape(-1, H)
        router_logits = hidden @ gate_w.T
        routing_weights = jax.nn.softmax(router_logits.astype(jnp.float32), axis=-1)
        topk_weights, topk_indices = jax.lax.top_k(routing_weights, top_k)
        topk_weights = topk_weights / (jnp.sum(topk_weights, axis=-1, keepdims=True) + EPS)
        N = hidden.shape[0]
        routed = jnp.zeros((N, E), dtype=router_logits.dtype)
        rows = jnp.arange(N)[:, None]
        routed = routed.at[rows, topk_indices].set(topk_weights.astype(router_logits.dtype))
        routed = routed / (jnp.sum(routed, axis=-1, keepdims=True) + EPS)
        routed = routed.astype(hidden.dtype)
        gate_up = jnp.einsum('th,ehq->teq', hidden, gate_up_proj)
        gate, up = jnp.split(gate_up, 2, axis=-1)
        expert_outputs = jnp.einsum('teq,eqh->teh', jax.nn.silu(gate) * up, down_proj)
        out = jnp.sum(expert_outputs * routed[:, :, None], axis=1)
        return out.reshape(B, T, H)
    x = x + _L0_xattn_ref(_layernorm(x, axis=-1), ctx_1024, ctx_1024, mask_SxS2_bk1, L0_xattn_q_w, L0_xattn_q_b, L0_xattn_k_w, L0_xattn_k_b, L0_xattn_v_w, L0_xattn_v_b, L0_xattn_o_w, L0_xattn_o_b)
    x = x + _L0_ffn_ref(_layernorm(x, axis=-1), L0_ffn_gate_w, L0_ffn_gate_up_proj, L0_ffn_down_proj)
    return x

_drawn_inputs = setup_inputs


def setup_inputs(seed=0):
    import zlib

    import numpy as np

    out = dict(_drawn_inputs(seed))
    spreads = {}
    factors = {'L0_xattn_q_b': 6.398, 'L0_xattn_k_b': 8.0}
    for name, (base, spread) in spreads.items():
        noise = np.random.default_rng([zlib.crc32(name.encode()), seed]).standard_normal(out[name].shape)
        drawn = base * np.exp(spread * noise) if base else spread * noise
        out[name] = jnp.asarray(drawn.astype(out[name].dtype))
    for name, factor in factors.items():
        out[name] = (out[name] * factor).astype(out[name].dtype)
    return out
```

```python
from contextlib import ExitStack

import concourse.bass as bass
from concourse import mybir

P = 128
F32 = mybir.dt.float32
F32R = mybir.dt.float32r
BF16 = mybir.dt.bfloat16
I32 = mybir.dt.int32
U32 = mybir.dt.uint32
U8 = mybir.dt.uint8
ALU = mybir.AluOpType
ACT = mybir.ActivationFunctionType
AX = mybir.AxisListType

B, S, D = 2, 2048, 512
KEYS, HEADS, HD = 77, 16, 32
KP = KEYS + 1
E, FF = 8, 512
LN_EPS, TOPK_EPS = 1e-5, 1e-9
C = D // P
HG = P // HD
J = HEADS // HG
GK = HG * KP
M = 3
MK = GK // M
VC = P + HG
TILES = B * S // P
GT = 4
GROUPS = TILES // GT
ROW = D + 1 + E
MINT = 3
REG = B * S + MINT * P
NOBODY = 8191
WCH = 6
MAXT = 2 * TILES + MINT * E
SCALE = 1.0 / float(HD) ** 0.5
MASKED = -1e30
assert GK % M == 0 and GK % 2 == 0


def build(nc, x, ctxT, mask, wq, q_b, wk, k_b, wv, v_b, wo, o_b, gw, gu, dn, out):
    with ExitStack() as ctx:
        def sb(name, shape, dt=F32):
            return ctx.enter_context(nc.sbuf_tensor(name, shape, dt))

        def sem(name):
            return ctx.enter_context(nc.semaphore(name))

        slots = nc.dram_tensor("slots", [E * REG, ROW], F32, kind="Internal").ap()
        xr_rows = x.rearrange("b s d -> (b s) d")
        out_rows = out.rearrange("b s d -> (b s) d")

        WE = C * (2 * FF) + C * D
        ops = sb("ops", [P, 4 * WE], F32R)
        CD = C * GT * P

        def part(at, inner):
            v = ops[:, at:at + 2 * CD].rearrange("p (h c n) -> p h c n", h=2, c=C)
            assert v.shape[3] == inner
            return v

        xT = [part(q * 2 * CD, 512) for q in range(2)]
        wq_s = part(4 * CD, D)
        qT = [part(6 * CD + q * 2 * CD, 512) for q in range(2)]
        wo_s = part(10 * CD, D)
        w_gu = [[ops[:, (2 * w + h) * WE:(2 * w + h) * WE + C * 2 * FF].rearrange("p (c n) -> p c n", c=C)
                 for h in range(2)] for w in range(2)]
        w_dn = [[ops[:, (2 * w + h) * WE + C * 2 * FF:(2 * w + h + 1) * WE].rearrange("p (c n) -> p c n", c=C)
                 for h in range(2)] for w in range(2)]
        kbd = sb("kbd", [P, 2 * B * J * GK], F32R)[:, :].rearrange("p (h b j n) -> p h b j n", h=2, b=B, j=J)
        kflat = kbd.rearrange("p h b j n -> p (h b j n)")
        vbd = sb("vbd", [P, 2 * B * J * M * VC], F32R)[:, :].rearrange(
            "p (h b j m n) -> p h b j m n", h=2, b=B, j=J, m=M)
        pT = sb("pT", [P, 2, 2, M * P], F32R)
        cT = sb("cT", [P, 2, C * P], F32R)
        rT = kflat[:, 0:2 * D].rearrange("p (h n) -> p h n", h=2)
        hT = cT

        stage = sb("stage", [P, WCH * 1024])
        xin = stage[:, 0:4 * D].rearrange("p (t n) -> p t n", t=4)
        SMW = HEADS * KP
        smx = stage[:, 4 * D:4 * D + 2 * SMW].rearrange("p (t n) -> p t n", t=2)
        c_at = 4 * D + 2 * SMW
        ctok = stage[:, c_at:c_at + 2 * D].rearrange("p (t n) -> p t n", t=2)
        h2T = stage[:, c_at + 2 * D:c_at + 3 * D]
        wraw = stage[:, :].rearrange("p (w n) -> p w n", w=WCH)
        xres = sb("xres", [P, 2, D])
        x2 = sb("x2", [P, 2, D])
        rows = sb("rows", [P, 2, GT, ROW])
        rflat = rows[:, :, :, :].rearrange("p q t n -> p (q t n)")
        mbias = sb("mbias", [P, S // P, KP], BF16)
        mraw = xres[:, 0, :].bitcast(U8)[:, 0:S // P * KP].rearrange("p (t n) -> p t n", n=KP)
        ident = sb("ident", [P, P])
        tri = sb("tri", [P, P], BF16)
        ones = sb("ones", [P, P], BF16)
        ones1 = sb("ones1", [1, P])
        gw_s = sb("gw_s", [P, C, E])
        qb_s = sb("qb_s", [P, J])
        kb_s = sb("kb_s", [P, J])
        vb_s = x2[0:1, 1, :]
        ob_s = sb("ob_s", [P, D])
        hsel = sb("hsel", [P, M, HG])
        toki = sb("toki", [P, TILES], U32)
        iota8i = sb("iota8i", [P, E], I32)
        iota8 = sb("iota8", [P, E])
        firsti = sb("firsti", [P, E], I32)
        first = sb("first", [P, E])
        mhalf = sb("mhalf", [P, 1])
        st1, mv1, ve1, rs1, nm1 = (sb(n, [P, 4, w]) for n, w in
                                   (("st1", 6), ("mv1", 2), ("ve1", 1), ("rs1", 1), ("nm1", 1)))
        st2, mv2, ve2, rs2, nm2 = (sb(n, [P, 4, w]) for n, w in
                                   (("st2", 6), ("mv2", 2), ("ve2", 1), ("rs2", 1), ("nm2", 1)))
        mxs = sb("mxs", [P, 2, HEADS])
        rden = sb("rden", [P, 2, 2, HG])
        lg = sb("lg", [P, 2, GT, E])
        top = sb("top", [P, GT, E])
        topi = sb("topi", [P, GT, E], U32)
        topf = sb("topf", [P, GT, 2])
        hot = sb("hot", [P, 2, GT, E])
        picked = sb("picked", [P, GT + 1, E], BF16)
        dif = sb("dif", [P, GT, E])
        ex = sb("ex", [P, GT, E])
        zs = sb("zs", [P, GT, 1])
        rz = sb("rz", [P, GT, 1])
        pp = sb("pp", [P, GT, 2])
        count = sb("count", [P, E])
        slot = sb("slot", [P, GT, E])
        tmp = sb("tmp", [P, GT, E])
        slotf = sb("slotf", [P, 2, GT])
        sloti = sb("sloti", [P, 2, 2, GT], U32)
        ntok = sb("ntok", [P, E], I32)
        ntile = sb("ntile", [P, E], I32)
        tbase = sb("tbase", [P, E + 1], I32)
        padrow = xres[:, :, :].rearrange("p t n -> p (t n)")[:, 0:ROW]
        rowb = rflat[:, 0:ROW]
        sg = xres[:, 0, :]
        hid = xres[:, 1, :]
        got = x2[:, 0, :]
        acc = x2[:, 1, :]
        meta = [sb(f"meta{n}", [P, 1 + E], U32) for n in range(3)]
        zero = sb("zero", [P, 1 + E], U32)
        idle = sb("idle", [P, 1], U32)

        bT, bQ, bS0, bS1, bP0, bP1, bV, bO = (
            ctx.enter_context(nc.psum_tensor(n, [P, 512], F32))
            for n in ("bT", "bQ", "bS0", "bS1", "bP0", "bP1", "bV", "bO"))
        bS, bP = [bS0, bS1], [bP0, bP1]

        names = """ld_wq ld_wo ld_wk ld_wv ld_ctx ld_mask ld_small mraw_set ctx_pad consts const_tiles
        cr_done wq_hi wq_lo wo_hi wo_lo kp kp_out kz k_hi k_lo vp v_tmp v_hi v_lo v_ones mask_done tok_done
        ln1 rs1d nm1d xn tx xh xl qp qh ql sp ma mxd sub ex_done pt ph pl pv rc cn tc ch cl op
        xb x2d ln2 rs2d nm2d hn th h2 rt lgd route dif_d exr hot_d rank
        counts pads zrow cchain
        rw whi wlo gt sgd th2 hh hl up hm tx2 rxh rxl dnp gat accd sct mshift m0""".split()
        s = {n: sem(n) for n in names}
        x_in = [sem(f"x_in{i}") for i in range(4)]
        xr_in = [sem(f"xr_in{i}") for i in range(2)]
        x_st = [sem(f"x_st{i}") for i in range(2)]
        scat = [sem(f"scat{i}") for i in range(GT)]
        w_in = [sem(f"w_in{i}") for i in range(WCH)]

        def rows_of(g, i):
            return (i // 2) * S + (2 * g + i % 2) * P

        block = ctx.enter_context(nc.Block())

        def has(t):
            return 0 <= t < TILES

        ROUTE_STEPS = 27
        STEPS = range(-9, TILES + 8)

        @block.sync
        def _(sp):
            sp.dma_start(stage[:, 0:4 * D].rearrange("p (c n) -> p c n", c=C),
                         wq).then_inc(s["ld_wq"], 16)
            sp.dma_start(stage[:, 4 * D:8 * D].rearrange("p (c n) -> p c n", c=C),
                         wo).then_inc(s["ld_wo"], 16)
            sp.dma_start(stage[:, 8 * D:12 * D].rearrange("p (c n) -> p c n", c=C),
                         wk).then_inc(s["ld_wk"], 16)
            sp.dma_start(rflat[:, 0:4 * D].rearrange("p (c n) -> p c n", c=C),
                         wv).then_inc(s["ld_wv"], 16)

            def load_x(t):
                g, i = t // GT, t % GT
                if t >= 4:
                    sp.wait_ge(s["tx"], t - 3)
                elif i == 0:
                    sp.wait_ge(s["wq_hi"], 1)
                    sp.wait_ge(s["wq_lo"], 1)
                sp.dma_start(xin[:, i, :], xr_rows[bass.ds(rows_of(g, i), P), :]).then_inc(x_in[i], 16)

            for t in range(4):
                load_x(t)
            for st in STEPS:
                if 4 <= st + 12 < TILES:
                    load_x(st + 12)
                if has(st):
                    i = st % GT
                    if st >= 2:
                        sp.wait_ge(s["x2d"], st - 1)
                    elif st == 0:
                        sp.wait_ge(s["v_lo"], 2 * M)
                    sp.dma_start(xres[:, st % 2, :], xr_rows[bass.ds(rows_of(st // GT, i), P), :]).then_inc(xr_in[st % 2], 16)
                if has(st - 2):
                    t = st - 2
                    sp.wait_ge(s["x2d"], t + 1)
                    sp.dma_start(out_rows[bass.ds(rows_of(t // GT, t % GT), P), :], x2[:, t % 2, :]).then_inc(x_st[t % 2], 16)

            def load_w(e, ch):
                n = e * WCH + ch
                if n >= WCH:
                    sp.wait_ge(s["wlo"], n - WCH + 1)
                if ch < 4:
                    src = gu[e, ch * P:(ch + 1) * P, :]
                    sp.dma_start(wraw[:, ch, :], src).then_inc(w_in[ch], 16)
                else:
                    src = dn[e].rearrange("(c p) n -> p c n", p=P)[:, 2 * (ch - 4):2 * (ch - 4) + 2, :]
                    sp.dma_start(wraw[:, ch, :].rearrange("p (c n) -> p c n", c=2), src).then_inc(w_in[ch], 16)

            sp.wait_ge(s["pt"], TILES * J)
            sp.wait_ge(s["tc"], TILES)
            sp.wait_ge(s["rt"], TILES)
            for ch in range(WCH):
                load_w(0, ch)
            sp.wait_ge(s["counts"], 1)
            sp.wait_ge(s["zrow"], 2)
            for e in range(E):
                n = sp.value_load(ntok[0:1, e:e + 1], min_val=0, max_val=B * S)
                sp.dma_start(slots[bass.ds(n + e * REG, MINT * P), :].rearrange("(k p) n -> p k n", p=P),
                             padrow[:, None, :].broadcast_to([P, MINT, ROW])).then_inc(s["pads"], 16)
            sp.wait_ge(s["pads"], 16 * E)
            for q in scat:
                sp.wait_ge(q, 16 * 2 * GROUPS)

            def load_rows(e, k, t):
                if not isinstance(t, int) or t > 0:
                    sp.wait_ge(s["tx2"], t)
                    sp.wait_ge(s["m0"], t)
                sp.dma_start(rowb, slots[bass.ds(k * P + e * REG, P), :]).then_inc(s["rw"], 16)

            for e in range(E):
                cnt = sp.value_load(ntile[0:1, e:e + 1], min_val=MINT, max_val=B * S // P)
                base = 1 + sp.value_load(tbase[0:1, e:e + 1], min_val=0, max_val=MAXT) if e else 0
                load_rows(e, 0, base)
                load_rows(e, 1, base + 1)
                if e + 1 < E:
                    for ch in range(WCH):
                        load_w(e + 1, ch)
                with sp.Fori(2, cnt) as k:
                    load_rows(e, k, base + k)
            tend = 1 + sp.value_load(tbase[0:1, E:E + 1], min_val=0, max_val=MAXT)
            load_rows(0, 0, tend)

        @block.gpsimd
        def _(pool):
            g_ = nc.gpsimd
            pool.dma_start(gw_s[:, :, :], gw).then_inc(s["ld_small"], 16)
            pool.dma_start(qb_s[:, :], q_b).then_inc(s["ld_small"], 16)
            pool.dma_start(kb_s[:, :], k_b).then_inc(s["ld_small"], 16)
            pool.dma_start(vb_s[:, :], v_b[None, :]).then_inc(s["ld_small"], 16)
            pool.dma_start(ob_s[:, :], o_b[None, :].broadcast_to([P, D])).then_inc(s["ld_small"], 16)
            g_.memset(ident[:, :], 0.0).then_inc(s["consts"], 1)
            g_.memset(tri[:, :], 1.0).then_inc(s["consts"], 1)
            g_.memset(hsel[:, :, :], 1.0).then_inc(s["consts"], 1)
            g_.memset(ones[:, :], 1.0).then_inc(s["const_tiles"], 1)
            g_.memset(ones1[:, :], 1.0).then_inc(s["const_tiles"], 1)
            g_.memset(mhalf[:, :], -0.5).then_inc(s["const_tiles"], 1)
            pool.wait_ge(s["consts"], 3)
            g_.affine_select(out=ident[:, :], in_=ident[:, :], compare_op=ALU.not_equal, fill=1.0, base=0,
                             pattern=[[-1, P]], channel_multiplier=1).then_inc(s["const_tiles"], 1)
            g_.affine_select(out=tri[:, :], in_=tri[:, :], compare_op=ALU.is_gt, fill=0.0, base=0,
                             pattern=[[1, P]], channel_multiplier=-1).then_inc(s["const_tiles"], 1)
            g_.affine_select(out=hsel[:, :, :], in_=hsel[:, :, :], compare_op=ALU.is_ge, fill=0.0, base=0,
                             pattern=[[MK, M], [-KP, HG]], channel_multiplier=1).then_inc(s["consts"], 1)
            pool.wait_ge(s["consts"], 4)
            g_.affine_select(out=hsel[:, :, :], in_=hsel[:, :, :], compare_op=ALU.is_ge, fill=0.0, base=KP - 1,
                             pattern=[[-MK, M], [KP, HG]], channel_multiplier=-1).then_inc(s["const_tiles"], 1)
            g_.iota(toki[:, :], pattern=[[2 * P, GROUPS], [S, 2], [P, 2]], base=0, channel_multiplier=1).then_inc(s["tok_done"], 1)
            g_.iota(iota8i[:, :], pattern=[[1, E]], base=0, channel_multiplier=0).then_inc(s["tok_done"], 1)
            g_.iota(firsti[:, :], pattern=[[REG, E]], base=0, channel_multiplier=0).then_inc(s["tok_done"], 1)
            g_.memset(picked[:, GT, :], 0.0).then_inc(s["const_tiles"], 1)

            def rstd(t, ve, rs, mv, nm, from_, rsd, nmd, per):
                i = t % 4
                pool.wait_ge(s[from_], per * t + per)
                g_.tensor_tensor(rs[:, i, :], ve[:, i, :], mhalf[:, :], ALU.pow).then_inc(s[rsd], 1)
                pool.wait_ge(s[rsd], t + 1)
                g_.tensor_scalar(nm[:, i, :], mv[:, i, 0:1], rs[:, i, 0:1], -1.0, ALU.mult, ALU.mult).then_inc(s[nmd], 1)

            for st in STEPS:
                if has(st - 3):
                    rstd(st - 3, ve2, rs2, mv2, nm2, "ln2", "rs2d", "nm2d", 3)
                if has(st - 1):
                    t = st - 1
                    if t == 0:
                        pool.wait_ge(s["ld_small"], 16 * 5)
                    pool.wait_ge(xr_in[t % 2], 16 * (t // 2 + 1))
                    g_.tensor_tensor(xres[:, t % 2, :], xres[:, t % 2, :], ob_s[:, :], ALU.add).then_inc(s["xb"], 1)
                if has(st + 9):
                    if st + 9 == 0:
                        pool.wait_ge(s["const_tiles"], 3)
                    rstd(st + 9, ve1, rs1, mv1, nm1, "ln1", "rs1d", "nm1d", 3)
                if has(st):
                    pool.wait_ge(s["mxd"], st + 1)
                    v = smx[:, st % 2, :].rearrange("p (h n) -> p h n", h=HEADS)
                    g_.tensor_tensor(v, v, mxs[:, st % 2, :, None].broadcast_to([P, HEADS, KP]),
                                     ALU.subtract).then_inc(s["sub"], 1)
                if has(st - 8):
                    g2, i = (st - 8) // GT, (st - 8) % GT
                    if i == 0:
                        pool.wait_ge(s["route"], ROUTE_STEPS * (g2 + 1))
                    if g2:
                        pool.wait_ge(scat[i], 16 * 2 * g2)
                    for k in range(2):
                        pool.indirect_dma_start(
                            out=slots[:, :], out_offset=bass.IndirectOffsetOnAxis(ap=sloti[:, g2 % 2, k, i:i + 1], axis=0),
                            in_=rows[:, g2 % 2, i, :], in_offset=None).then_inc(scat[i], 16)

            for q in x_st:
                pool.wait_ge(q, 16 * TILES // 2)
            g_.memset(padrow[:, :], 0.0).then_inc(s["zrow"], 1)
            pool.wait_ge(s["zrow"], 1)
            g_.memset(padrow[:, D:D + 1].bitcast(U32), NOBODY).then_inc(s["zrow"], 1)
            g_.memset(got, 0.0).then_inc(s["zrow"], 1)
            pool.wait_ge(s["zrow"], 3)


            def combine(t):
                pool.indirect_dma_start(
                    out=got, out_offset=None, in_=out_rows[:, :],
                    in_offset=bass.IndirectOffsetOnAxis(ap=meta[2][:, 0:1], axis=0),
                    bounds_check=B * S - 1, oob_is_err=False).then_inc(s["gat"], 16)
                pool.wait_ge(s["accd"], t + 1)
                g_.tensor_tensor(idle[:, :], zero[:, 0:1], zero[:, 0:1], ALU.add)
                pool.indirect_dma_start(
                    out=out_rows[:, :], out_offset=bass.IndirectOffsetOnAxis(ap=meta[2][:, 0:1], axis=0),
                    in_=acc, in_offset=None,
                    bounds_check=B * S - 1, oob_is_err=False).then_inc(s["sct"], 16)
                pool.wait_ge(s["sct"], 16 * t + 16)

            def move(to, of):
                return g_.tensor_tensor(meta[to][:, :], meta[of][:, :], zero[:, :], ALU.add)

            def shift(t):
                pool.wait_ge(s["m0"], t + 2)
                move(2, 1).then_inc(s["mshift"], 1)
                pool.wait_ge(s["mshift"], 2 * t + 1)
                move(1, 0).then_inc(s["mshift"], 1)

            pool.wait_ge(s["m0"], 1)
            g_.memset(zero[:, :], 0).then_inc(s["zrow"], 1)
            pool.wait_ge(s["zrow"], 4)
            move(1, 0).then_inc(s["zrow"], 1)
            pool.wait_ge(s["counts"], 1)
            for e in range(E):
                cnt = pool.value_load(ntile[0:1, e:e + 1], min_val=MINT, max_val=B * S // P)
                base = 1 + pool.value_load(tbase[0:1, e:e + 1], min_val=0, max_val=MAXT) if e else 0
                with pool.Fori(0, cnt) as k:
                    shift(base + k)
                    combine(base + k)
            tend = 1 + pool.value_load(tbase[0:1, E:E + 1], min_val=0, max_val=MAXT)
            pool.wait_ge(s["sct"], 16 * tend)

        @block.scalar
        def _(act):
            a = nc.scalar

            def copy(o, i):
                return a.activation(o, i, ACT.Copy)

            cx = rflat[:, 4 * D:4 * D + C * B * KP].rearrange("p (c b n) -> p c b n", c=C, b=B)
            def ph(t, j):
                n = 4 * t + j
                act.wait_ge(s["pt"], n + 1)
                if n >= 2:
                    act.wait_ge(s["pv"], n - 1)
                copy(pT[0:MK, j % 2, 0, :], bP[j % 2][0:MK, 0:M * P]).then_inc(s["ph"], 1)

            act.wait_ge(s["ctx_pad"], 1)
            for b in range(B):
                act.dma_start(cx[:, :, b, 0:KEYS], ctxT[b]).then_inc(s["ld_ctx"], 16)
            act.wait_ge(s["mraw_set"], 1)
            act.dma_start(mraw[:, :, 0:KEYS], mask).then_inc(s["ld_mask"], 16)
            act.wait_ge(s["ld_wq"], 16)
            copy(wq_s[:, 0].rearrange("p c n -> p (c n)"), stage[:, 0:4 * D]).then_inc(s["wq_hi"], 1)
            act.wait_ge(s["ld_wo"], 16)
            copy(wo_s[:, 0].rearrange("p c n -> p (c n)"), stage[:, 4 * D:8 * D]).then_inc(s["wo_hi"], 1)
            act.wait_ge(s["ld_small"], 16 * 5)
            ktmp = x2[:, 0, 0:B * KEYS].rearrange("p (b n) -> p b n", b=B)
            for j in range(J):
                act.wait_ge(s["kp"], j + 1)
                if j >= 1:
                    act.wait_ge(s["k_lo"], HG * j)
                a.activation(ktmp, bP[0][:, 0:B * KEYS].rearrange("p (b n) -> p b n", b=B), ACT.Identity,
                             bias=kb_s[:, j:j + 1]).then_inc(s["kp_out"], 1)
                act.wait_ge(s["kp_out"], j + 1)
                if j == 0:
                    act.wait_ge(s["kz"], 1)
                for h in range(HG):
                    rs = slice(h * HD, (h + 1) * HD)
                    copy(kbd[rs, 0, :, j, h * KP:h * KP + KEYS], ktmp[rs]).then_inc(s["k_hi"], 1)
            for n in range(B * M):
                b, m = n // M, n % M
                act.wait_ge(s["v_tmp"], n + 1)
                vt = xres[0:MK, n % 2, :].rearrange("p (j n) -> p j n", j=J)
                copy(vbd[0:MK, 0, b, :, m, 0:P], vt).then_inc(s["v_hi"], 1)

            def norm(t, dst, src, rs, nm):
                i = t % 4
                return a.activation(dst, src, ACT.Identity, scale=rs[:, i, 0:1], bias=nm[:, i, 0:1])

            for st in STEPS:
                g, i = st // GT, st % GT
                if has(st - 1):
                    ph(st - 1, 0)
                if has(st + 8):
                    t = st + 8
                    act.wait_ge(s["tx"], t + 1)
                    if t >= 8 and t % GT == 0:
                        act.wait_ge(s["qp"], 4 * (t // GT - 1))
                    copy(xT[(t // GT) % 2][:, 0, :, (t % GT) * P:(t % GT + 1) * P],
                         bT[:, :].rearrange("p (c n) -> p c n", c=C)).then_inc(s["xh"], 1)
                if has(st - 1):
                    ph(st - 1, 1)
                gq = g + 1
                if 0 <= gq < GROUPS:
                    act.wait_ge(s["qp"], 4 * gq + i + 1)
                    if gq >= 2 and i == 0:
                        act.wait_ge(s["sp"], 16 * (gq - 1))
                    a.activation(qT[gq % 2][:, 0, i, :], bQ[:, :], ACT.Identity,
                                 bias=qb_s[:, i:i + 1]).then_inc(s["qh"], 1)
                if has(st - 3):
                    t = st - 3
                    act.wait_ge(s["nm2d"], t + 1)
                    act.wait_ge(s["x2d"], t + 1)
                    if t >= 2 * GT:
                        act.wait_ge(scat[t % GT], 16 * 2 * (t // GT - 1))
                    norm(t, rows[:, (t // GT) % 2, t % GT, 0:D], x2[:, t % 2, :], rs2, nm2).then_inc(s["hn"], 1)
                if has(st - 2):
                    t = st - 2
                    act.wait_ge(s["tc"], t + 1)
                    if t >= 1:
                        act.wait_ge(s["op"], t)
                    copy(cT[:, 0, :], bT[:, :]).then_inc(s["ch"], 1)
                if has(st - 1):
                    ph(st - 1, 2)
                    ph(st - 1, 3)
                if has(st):
                    act.wait_ge(s["sub"], st + 1)
                    a.activation(smx[:, st % 2, :], smx[:, st % 2, :], ACT.Exp, scale=SCALE).then_inc(s["ex_done"], 1)
                if has(st - 3):
                    act.wait_ge(s["th"], st - 2)
                    if st - 3 >= 1:
                        act.wait_ge(s["rt"], st - 3)
                    copy(h2T, bT[:, :]).then_inc(s["h2"], 1)
                if has(st + 9):
                    t = st + 9
                    act.wait_ge(s["nm1d"], t + 1)
                    norm(t, xin[:, t % 4, :], xin[:, t % 4, :], rs1, nm1).then_inc(s["xn"], 1)
                gr = (st - 6) // GT
                if (st - 6) % GT == 0 and 0 <= gr < GROUPS:
                    act.wait_ge(s["dif_d"], gr + 1)
                    a.activation(ex[:, :, :], dif[:, :, :], ACT.Exp).then_inc(s["exr"], 1)

            def split_hi(e, ch):
                n = e * WCH + ch
                act.wait_ge(w_in[ch], 16 * (e + 1))
                w = e % 2
                dst = (w_gu[w][0][:, ch, :] if ch < 4 else
                       w_dn[w][0][:, 2 * (ch - 4):2 * (ch - 4) + 2, :].rearrange("p c n -> p (c n)"))
                copy(dst, wraw[:, ch, :]).then_inc(s["whi"], 1)

            act.wait_ge(s["qp"], 4 * GROUPS)
            for ch in range(WCH):
                split_hi(0, ch)
            act.wait_ge(s["op"], TILES)
            act.wait_ge(s["counts"], 1)

            def silu(t):
                act.wait_ge(s["gt"], t + 1)
                if not isinstance(t, int) or t > 0:
                    act.wait_ge(s["hm"], t)
                a.activation(sg, bS0[:, :], ACT.Silu).then_inc(s["sgd"], 1)

            def hidden_hi(p):
                act.wait_ge(s["th2"], p + 1)
                if not isinstance(p, int) or p > 0:
                    act.wait_ge(s["dnp"], p)
                copy(hT[:, 0, :], bT[:, :]).then_inc(s["hh"], 1)

            def rows_hi(t):
                act.wait_ge(s["tx2"], t + 1)
                if not isinstance(t, int) or t > 0:
                    act.wait_ge(s["up"], t)
                copy(rT[:, 0, :], bQ[:, :]).then_inc(s["rxh"], 1)

            rows_hi(0)
            for e in range(E):
                cnt = act.value_load(ntile[0:1, e:e + 1], min_val=MINT, max_val=B * S // P)
                before = act.value_load(tbase[0:1, e:e + 1], min_val=0, max_val=MAXT) if e else -1
                for k in range(2):
                    p = before + k
                    silu(p + 1)
                    if e or k:
                        hidden_hi(p)
                    rows_hi(p + 2)
                    if e + 1 < E:
                        if k == 0 and e:
                            act.wait_ge(s["dnp"], p + 1)
                        for ch in range(3 * k, 3 * k + 3):
                            split_hi(e + 1, ch)
                with act.Fori(1, cnt - 1) as k:
                    p = before + 1 + k
                    silu(p + 1)
                    hidden_hi(p)
                    rows_hi(p + 2)
            last = act.value_load(tbase[0:1, E:E + 1], min_val=0, max_val=MAXT)
            hidden_hi(last)

        @block.vector
        def _(dve):
            v = nc.vector

            def f(ap):
                return ap.bitcast(F32)

            def lo(dst, full, hi):
                return v.tensor_tensor(dst, full, f(hi), ALU.subtract)

            cx = rflat[:, 4 * D:4 * D + C * B * KP].rearrange("p (c b n) -> p c b n", c=C, b=B)
            cr = rflat[:, 4 * D + C * B * KP:4 * D + C * B * KP + C * GK].rearrange("p (c h n) -> p c h n", c=C, h=HG)
            v.memset(rflat[:, 4 * D:4 * D + C * B * KP], 0.0).then_inc(s["ctx_pad"], 1)
            v.memset(mraw[:, :, :], 1).then_inc(s["mraw_set"], 1)
            v.memset(f(kflat), 0.0).then_inc(s["kz"], 1)
            v.memset(f(vbd[:, 1, :, :, :, :].rearrange("p b j m n -> p (b j m n)")), 0.0).then_inc(s["kz"], 1)
            dve.wait_ge(s["wq_hi"], 1)
            lo(wq_s[:, 1].rearrange("p c n -> p (c n)"), stage[:, 0:4 * D],
               wq_s[:, 0].rearrange("p c n -> p (c n)")).then_inc(s["wq_lo"], 1)
            dve.wait_ge(s["tok_done"], 3)
            v.tensor_copy(iota8[:, :], iota8i[:, :]).then_inc(s["tok_done"], 1)
            v.tensor_copy(count[:, :], firsti[:, :]).then_inc(s["tok_done"], 1)
            v.tensor_copy(first[:, :], firsti[:, :]).then_inc(s["tok_done"], 1)
            dve.wait_ge(s["ld_mask"], 16)
            v.tensor_scalar(mbias[:, :, :], mraw[:, :, :], MASKED, None, ALU.mult).then_inc(s["mask_done"], 1)

            def ln(t, src, stt, mv, ve, name):
                i = t % 4
                v.bn_stats(stt[:, i, :], src).then_inc(s[name], 1)
                dve.wait_ge(s[name], 3 * t + 1)
                v.bn_aggr(mv[:, i, :], stt[:, i, :]).then_inc(s[name], 1)
                dve.wait_ge(s[name], 3 * t + 2)
                v.tensor_scalar(ve[:, i, :], mv[:, i, 1:2], LN_EPS, None, ALU.add).then_inc(s[name], 1)

            def ln_x(t):
                dve.wait_ge(x_in[t % 4], 16 * (t // 4 + 1))
                ln(t, xin[:, t % 4, :], st1, mv1, ve1, "ln1")

            dve.wait_ge(s["ld_ctx"], 16 * B)
            for b in range(B):
                if b:
                    dve.wait_ge(s["vp"], M * b)
                for c in range(C):
                    r = v.tensor_copy(cr[:, c], cx[:, c, b, None, :].broadcast_to([P, HG, KP]))
                r.then_inc(s["cr_done"], 1)
                if b == 0:
                    ktmp = x2[:, 0, 0:B * KEYS].rearrange("p (b n) -> p b n", b=B)
                    for j in range(J):
                        for h in range(HG):
                            rs = slice(h * HD, (h + 1) * HD)
                            dve.wait_ge(s["k_hi"], HG * j + h + 1)
                            lo(kbd[rs, 1, :, j, h * KP:h * KP + KEYS], ktmp[rs],
                               kbd[rs, 0, :, j, h * KP:h * KP + KEYS]).then_inc(s["k_lo"], 1)
                    dve.wait_ge(s["const_tiles"], 7)
                for m in range(M):
                    n = b * M + m
                    dve.wait_ge(s["vp"], n + 1)
                    vt = xres[0:MK, n % 2, :].rearrange("p (j n) -> p j n", j=J)
                    for j in range(J):
                        r = v.tensor_tensor(vt[:, j].rearrange("p (h n) -> p h n", h=HG),
                                            bP[n % 2][0:MK, j * P:(j + 1) * P].rearrange("p (h n) -> p h n", h=HG),
                                            hsel[0:MK, m, :, None].broadcast_to([MK, HG, HD]), ALU.mult)
                    r.then_inc(s["v_tmp"], 1)
                    v.tensor_copy(vbd[0:MK, 0, b, :, m, P:VC],
                                  hsel[0:MK, m, None, :].broadcast_to([MK, J, HG])).then_inc(s["v_ones"], 1)
                    dve.wait_ge(s["v_hi"], n + 1)
                    lo(vbd[0:MK, 1, b, :, m, 0:P], vt, vbd[0:MK, 0, b, :, m, 0:P]).then_inc(s["v_lo"], 1)
            dve.wait_ge(s["wo_hi"], 1)
            lo(wo_s[:, 1].rearrange("p c n -> p (c n)"), stage[:, 4 * D:8 * D],
               wo_s[:, 0].rearrange("p c n -> p (c n)")).then_inc(s["wo_lo"], 1)

            def pl(t, j):
                dve.wait_ge(s["ph"], 4 * t + j + 1)
                lo(pT[0:MK, j % 2, 1, :], bP[j % 2][0:MK, 0:M * P], pT[0:MK, j % 2, 0, :]).then_inc(s["pl"], 1)

            def mask_add(t, j):
                dve.wait_ge(s["sp"], 4 * t + j + 1)
                if t >= 2 and j == 0:
                    dve.wait_ge(s["pt"], 4 * (t - 1))
                if t == 0 and j == 0:
                    dve.wait_ge(s["wo_lo"], 1)
                    dve.wait_ge(s["kp"], J)
                g, i = t // GT, t % GT
                mt = 2 * g + i % 2
                v.tensor_tensor(smx[:, t % 2, j * GK:(j + 1) * GK].rearrange("p (h n) -> p h n", h=HG),
                                bS[j % 2][:, 0:GK].rearrange("p (h n) -> p h n", h=HG),
                                mbias[:, bass.ds(mt, 1), :].broadcast_to([P, HG, KP]), ALU.add).then_inc(s["ma"], 1)

            def context(t, h):
                dve.wait_ge(s["pv"], 4 * t + 2 * h + 2)
                pvv = bV[:, 0:2 * VC].rearrange("p (j n) -> p j n", j=2)
                v.reciprocal(rden[:, h], pvv[:, :, P:VC]).then_inc(s["rc"], 1)
                dve.wait_ge(s["rc"], 2 * t + h + 1)
                if t >= 2 and h == 0:
                    dve.wait_ge(s["tc"], t - 1)
                v.tensor_tensor(ctok[:, t % 2, h * 256:(h + 1) * 256].rearrange("p (j h n) -> p j h n", j=2, h=HG),
                                pvv[:, :, 0:P].rearrange("p j (h n) -> p j h n", h=HG),
                                rden[:, h, :, :, None].broadcast_to([P, 2, HG, HD]), ALU.mult).then_inc(s["cn"], 1)

            def route_1(g):
                n = [ROUTE_STEPS * g]

                def link(ins):
                    n[0] += 1
                    ins.then_inc(s["route"], 1)
                    dve.wait_ge(s["route"], n[0])

                for i in range(GT):
                    r = v.max(top[:, i, :], lg[:, g % 2, i, :])
                    if i == GT - 1:
                        link(r)
                    else:
                        r.then_inc(s["route"], 1)
                        n[0] += 1
                for i in range(GT):
                    r = v.max_index(topi[:, i, :], top[:, i, :], lg[:, g % 2, i, :])
                    if i == GT - 1:
                        link(r)
                    else:
                        r.then_inc(s["route"], 1)
                        n[0] += 1
                v.tensor_tensor(dif[:, :, :], top[:, :, :], top[:, :, 0:1].broadcast_to([P, GT, E]),
                                ALU.subtract).then_inc(s["dif_d"], 1)
                link(v.tensor_copy(topf[:, :, :], topi[:, :, 0:2]))
                for k in range(2):
                    r = v.tensor_tensor(hot[:, k], iota8[:, None, :].broadcast_to([P, GT, E]),
                                        topf[:, :, k:k + 1].broadcast_to([P, GT, E]), ALU.is_equal)
                link(r)
                v.tensor_tensor(picked[:, 0:GT, :], hot[:, 0], hot[:, 1], ALU.add).then_inc(s["hot_d"], 1)
                return n[0]

            def route_2(g, at):
                n = [at]

                def link(ins):
                    n[0] += 1
                    ins.then_inc(s["route"], 1)
                    dve.wait_ge(s["route"], n[0])

                q = g % 2
                dve.wait_ge(s["exr"], g + 1)
                link(v.tensor_reduce(zs[:, :, 0], ex[:, :, :], AX.X, ALU.add))
                link(v.reciprocal(rz[:, :, 0], zs[:, :, 0]))
                link(v.tensor_tensor(pp[:, :, :], ex[:, :, 0:2], rz[:, :, :].broadcast_to([P, GT, 2]), ALU.mult))
                for _ in range(2):
                    link(v.scalar_tensor_tensor(zs[:, :, 0], pp[:, :, 0], TOPK_EPS, pp[:, :, 1], ALU.add, ALU.add))
                    link(v.reciprocal(rz[:, :, 0], zs[:, :, 0]))
                    link(v.tensor_tensor(pp[:, :, :], pp[:, :, :], rz[:, :, :].broadcast_to([P, GT, 2]), ALU.mult))
                link(v.tensor_tensor(tmp[:, :, :], hot[:, 0], pp[:, :, 0:1].broadcast_to([P, GT, E]), ALU.mult))
                link(v.tensor_tensor(slot[:, :, :], hot[:, 1], pp[:, :, 1:2].broadcast_to([P, GT, E]), ALU.mult))
                v.tensor_tensor(rows[:, q, :, D + 1:ROW], tmp[:, :, :], slot[:, :, :], ALU.add)
                link(v.tensor_copy(rows[:, q, :, D].bitcast(U32), toki[:, bass.ds(g * GT, GT)]))
                dve.wait_ge(s["rank"], g + 1)
                v.tensor_tensor(slot[:, :, :], bT[:, 0:GT * E].rearrange("p (t e) -> p t e", t=GT),
                                count[:, None, :].broadcast_to([P, GT, E]), ALU.add).then_inc(s["hot_d"], 1)
                dve.wait_ge(s["hot_d"], 3 * g + 2)
                v.tensor_tensor(count[:, :], count[:, :], bT[:, GT * E:GT * E + E], ALU.add).then_inc(s["hot_d"], 1)
                for k in range(2):
                    link(v.tensor_tensor(tmp[:, :, :], slot[:, :, :], hot[:, k], ALU.mult))
                    link(v.tensor_reduce(slotf[:, k, :], tmp[:, :, :], AX.X, ALU.add))
                v.tensor_copy(sloti[:, q, :, :], slotf[:, :, :]).then_inc(s["route"], 1)
                assert n[0] + 1 == ROUTE_STEPS * (g + 1)

            at = 0
            for st in STEPS:
                g, i = st // GT, st % GT
                if has(st):
                    mask_add(st, 0)
                    mask_add(st, 1)
                if has(st - 1):
                    pl(st - 1, 0)
                if has(st + 8):
                    t = st + 8
                    dve.wait_ge(s["xh"], t + 1)
                    cs = slice((t % GT) * P, (t % GT + 1) * P)
                    lo(xT[(t // GT) % 2][:, 1, :, cs], bT[:, :].rearrange("p (c n) -> p c n", c=C),
                       xT[(t // GT) % 2][:, 0, :, cs]).then_inc(s["xl"], 1)
                if has(st):
                    mask_add(st, 2)
                if has(st - 1):
                    pl(st - 1, 1)
                if has(st):
                    mask_add(st, 3)
                    dve.wait_ge(s["ma"], 4 * st + 4)
                    v.tensor_reduce(mxs[:, st % 2, :], smx[:, st % 2, :].rearrange("p (h n) -> p h n", h=HEADS),
                                    AX.X, ALU.max).then_inc(s["mxd"], 1)
                if has(st + 9):
                    ln_x(st + 9)
                gq = g + 1
                if 0 <= gq < GROUPS:
                    dve.wait_ge(s["qh"], 4 * gq + i + 1)
                    v.scalar_tensor_tensor(qT[gq % 2][:, 1, i, :], bQ[:, :], qb_s[:, i:i + 1], f(qT[gq % 2][:, 0, i, :]),
                                           ALU.add, ALU.subtract).then_inc(s["ql"], 1)
                if has(st - 2):
                    dve.wait_ge(s["ch"], st - 1)
                    lo(cT[:, 1, :], bT[:, :], cT[:, 0, :]).then_inc(s["cl"], 1)
                if has(st - 1):
                    context(st - 1, 0)
                    pl(st - 1, 2)
                    pl(st - 1, 3)
                if has(st - 2):
                    t = st - 2
                    dve.wait_ge(s["op"], t + 1)
                    dve.wait_ge(s["xb"], t + 1)
                    if t >= 2:
                        dve.wait_ge(x_st[t % 2], 16 * (t // 2))
                        dve.wait_ge(s["hn"], t - 1)
                    v.tensor_tensor(x2[:, t % 2, :], bO[:, :], xres[:, t % 2, :], ALU.add).then_inc(s["x2d"], 1)
                    dve.wait_ge(s["x2d"], t + 1)
                    ln(t, x2[:, t % 2, :], st2, mv2, ve2, "ln2")
                if has(st - 1):
                    context(st - 1, 1)
                if has(st - 3):
                    t = st - 3
                    dve.wait_ge(s["rt"], t + 1)
                    v.tensor_copy(lg[:, (t // GT) % 2, t % GT, :], bT[:, 0:E]).then_inc(s["lgd"], 1)
                    dve.wait_ge(s["lgd"], t + 1)
                gr = (st - 6) // GT
                if (st - 6) % GT == 0 and 0 <= gr < GROUPS:
                    at = route_1(gr)
                gr = (st - 7) // GT
                if (st - 7) % GT == 0 and 0 <= gr < GROUPS:
                    route_2(gr, at)

            dve.wait_ge(s["hot_d"], 3 * GROUPS)
            v.tensor_tensor(ntok[:, :], count[:, :], first[:, :], ALU.subtract).then_inc(s["cchain"], 1)
            dve.wait_ge(s["cchain"], 1)
            v.tensor_scalar(ntile[:, :], ntok[:, :], float(P - 1), None, ALU.add).then_inc(s["cchain"], 1)
            dve.wait_ge(s["cchain"], 2)
            v.tensor_scalar(ntile[:, :], ntile[:, :], 7, None, ALU.logical_shift_right).then_inc(s["cchain"], 1)
            dve.wait_ge(s["cchain"], 3)
            v.tensor_scalar(ntile[:, :], ntile[:, :], float(MINT), None, ALU.max).then_inc(s["cchain"], 1)
            v.memset(tbase[:, 0:1], -1).then_inc(s["cchain"], 1)
            for e in range(E):
                dve.wait_ge(s["cchain"], 5 + e)
                v.tensor_tensor(tbase[:, e + 1:e + 2], tbase[:, e:e + 1], ntile[:, e:e + 1], ALU.add).then_inc(s["cchain"], 1)
            dve.wait_ge(s["cchain"], 5 + E)
            v.memset(zs[:, :, :], 0.0).then_inc(s["counts"], 1)

            def split_lo(e, ch):
                n = e * WCH + ch
                dve.wait_ge(s["whi"], n + 1)
                w = e % 2

                def at_(h):
                    return (w_gu[w][h][:, ch, :] if ch < 4 else
                            w_dn[w][h][:, 2 * (ch - 4):2 * (ch - 4) + 2, :].rearrange("p c n -> p (c n)"))
                lo(at_(1), wraw[:, ch, :], at_(0)).then_inc(s["wlo"], 1)

            for ch in range(WCH):
                split_lo(0, ch)

            def rows_lo(p):
                dve.wait_ge(s["rxh"], p + 3)
                lo(rT[:, 1, :], bQ[:, :], rT[:, 0, :]).then_inc(s["rxl"], 1)
                if not isinstance(p, int) or p > -1:
                    dve.wait_ge(s["mshift"], 2 * p + 2)
                elif p == -1:
                    dve.wait_ge(s["zrow"], 5)
                v.tensor_copy(meta[0][:, :], rowb[:, D:ROW].bitcast(U32)).then_inc(s["m0"], 1)

            def hidden_lo(p):
                dve.wait_ge(s["hh"], p + 1)
                lo(hT[:, 1, :], bT[:, :], hT[:, 0, :]).then_inc(s["hl"], 1)

            def hidden(t):
                dve.wait_ge(s["sgd"], t + 1)
                dve.wait_ge(s["up"], t + 1)
                dve.wait_ge(s["th2"], t) if not isinstance(t, int) or t > 0 else None
                v.tensor_tensor(hid, bS1[:, :], sg, ALU.mult).then_inc(s["hm"], 1)

            def accumulate(e, p):
                dve.wait_ge(s["dnp"], p + 1)
                dve.wait_ge(s["gat"], 16 * p + 16)
                v.scalar_tensor_tensor(acc, bO[:, :], meta[2][:, 1 + e:2 + e].bitcast(F32), got, ALU.mult, ALU.add).then_inc(s["accd"], 1)

            rows_lo(-2)
            for e in range(E):
                cnt = dve.value_load(ntile[0:1, e:e + 1], min_val=MINT, max_val=B * S // P)
                before = dve.value_load(tbase[0:1, e:e + 1], min_val=0, max_val=MAXT) if e else -1
                for k in range(2):
                    p = before + k
                    if e or k:
                        hidden_lo(p)
                    hidden(p + 1)
                    rows_lo(p)
                    if e or k:
                        accumulate(e if k else e - 1, p)
                    if e + 1 < E:
                        for ch in range(3 * k, 3 * k + 3):
                            split_lo(e + 1, ch)
                with dve.Fori(1, cnt - 1) as k:
                    p = before + 1 + k
                    hidden_lo(p)
                    hidden(p + 1)
                    rows_lo(p)
                    accumulate(e, p)
            last = dve.value_load(tbase[0:1, E:E + 1], min_val=0, max_val=MAXT)
            hidden_lo(last)
            accumulate(E - 1, last)

        @block.tensor
        def _(pe):
            te = nc.tensor

            def three(o, ws, xs, n):
                for c in range(n):
                    for at, (a, b) in enumerate(((0, 0), (0, 1), (1, 0))):
                        r = te.matmul(o, ws(a, c), xs(b, c), start=(c == 0 and at == 0),
                                      stop=(c == n - 1 and at == 2))
                return r

            def transposes(bank, src):
                for c in range(C):
                    r = te.transpose(bank[:, c * P:(c + 1) * P], src[:, c * P:(c + 1) * P], ident[:, :])
                return r

            cx = rflat[:, 4 * D:4 * D + C * B * KP].rearrange("p (c b n) -> p c b n", c=C, b=B)
            cr = rflat[:, 4 * D + C * B * KP:4 * D + C * B * KP + C * GK].rearrange("p (c n) -> p c n", c=C)
            wk_r = stage[:, 8 * D:12 * D].rearrange("p (c n) -> p c n", c=C)
            wv_r = rflat[:, 0:4 * D].rearrange("p (c n) -> p c n", c=C)
            pe.wait_ge(s["ld_wk"], 16)
            pe.wait_ge(s["ld_ctx"], 16 * B)
            for j in range(J):
                if j:
                    pe.wait_ge(s["kp_out"], j)
                for c in range(C):
                    r = te.matmul(bP[0][:, 0:B * KEYS].rearrange("p (b n) -> p b n", b=B),
                                  wk_r[:, c, j * P:(j + 1) * P], cx[:, c, :, 0:KEYS], start=(c == 0), stop=(c == C - 1))
                r.then_inc(s["kp"], 1)
            pe.wait_ge(s["ld_wv"], 16)
            pe.wait_ge(s["ld_small"], 16 * 5)
            pe.wait_ge(s["const_tiles"], 7)
            pe.wait_ge(s["kp_out"], J)
            for n in range(B * M):
                b, m = n // M, n % M
                pe.wait_ge(s["cr_done"], b + 1)
                if n >= 2:
                    pe.wait_ge(s["v_tmp"], n - 1)
                te.matmul(bP[n % 2][0:MK, :], ones1[0:1, 0:MK], vb_s[0:1, :], start=True, stop=False)
                for c in range(C):
                    r = te.matmul(bP[n % 2][0:MK, :], cr[:, c, m * MK:(m + 1) * MK], wv_r[:, c, :],
                                  start=False, stop=(c == C - 1))
                r.then_inc(s["vp"], 1)
            pe.wait_ge(s["v_tmp"], B * M)

            def scores(t, j):
                g, b = t // GT, (t % GT) // 2
                if t % GT == 0 and j == 0:
                    pe.wait_ge(s["ql"], 4 * (g + 1))
                if t == 0 and j == 0:
                    pe.wait_ge(s["k_lo"], J * HG)
                n = 4 * t + j
                if n >= 2:
                    pe.wait_ge(s["ma"], n - 1)
                cs = slice((t % GT) * P, (t % GT + 1) * P)
                q = qT[g % 2]
                three(bS[j % 2][:, 0:GK], lambda h, c: q[:, h, j, cs], lambda h, c: kbd[:, h, b, j, :], 1).then_inc(s["sp"], 1)

            def probs_T(t, j):
                n = 4 * t + j
                if j == 0:
                    pe.wait_ge(s["ex_done"], t + 1)
                if n >= 2:
                    pe.wait_ge(s["pl"], n - 1)
                for m in range(M):
                    at = j * GK + m * MK
                    r = te.transpose(bP[j % 2][0:MK, m * P:(m + 1) * P], smx[:, t % 2, at:at + MK], ident[:, :])
                r.then_inc(s["pt"], 1)

            def values(t, j):
                b = (t % GT) // 2
                pe.wait_ge(s["pl"], 4 * t + j + 1)
                if j % 2 == 0 and (t or j):
                    pe.wait_ge(s["cn"], 2 * t + j // 2)
                if t == 0 and j == 0:
                    pe.wait_ge(s["v_lo"], B * M)
                three(bV[:, (j % 2) * VC:(j % 2 + 1) * VC],
                      lambda h, m: pT[0:MK, j % 2, h, m * P:(m + 1) * P],
                      lambda h, m: vbd[0:MK, h, b, j, m, :], M).then_inc(s["pv"], 1)

            for st in STEPS:
                g, i = st // GT, st % GT
                if has(st):
                    scores(st, 0)
                    scores(st, 1)
                if has(st - 1):
                    probs_T(st - 1, 0)
                if has(st + 8):
                    t = st + 8
                    if t == 0:
                        pe.wait_ge(s["const_tiles"], 7)
                    pe.wait_ge(s["xn"], t + 1)
                    if st - 4 >= 0:
                        pe.wait_ge(s["lgd"], st - 3)
                    if (st - 8) % GT == 0 and st - 8 >= 0:
                        pe.wait_ge(s["hot_d"], 3 * ((st - 8) // GT + 1))
                    if t >= 1:
                        pe.wait_ge(s["xl"], t)
                    transposes(bT, xin[:, t % 4, :]).then_inc(s["tx"], 1)
                if has(st):
                    scores(st, 2)
                if has(st - 1):
                    probs_T(st - 1, 1)
                if has(st):
                    scores(st, 3)
                gq = g + 1
                if 0 <= gq < GROUPS:
                    if i == 0:
                        pe.wait_ge(s["xl"], 4 * gq + 4)
                    if gq == 0 and i == 0:
                        pe.wait_ge(s["wq_lo"], 1)
                    if gq or i:
                        pe.wait_ge(s["ql"], 4 * gq + i)
                    xx = xT[gq % 2]
                    three(bQ[:, :], lambda h, c: wq_s[:, h, c, i * P:(i + 1) * P], lambda h, c: xx[:, h, c, :], C).then_inc(s["qp"], 1)
                if has(st - 2):
                    t = st - 2
                    pe.wait_ge(s["cn"], 2 * t + 2)
                    pe.wait_ge(s["xl"], min(TILES, st + 9))
                    if not has(st + 8):
                        pe.wait_ge(s["lgd"], st - 3) if st - 3 > 0 else None
                        if (st - 8) % GT == 0 and st - 8 >= 0:
                            pe.wait_ge(s["hot_d"], 3 * ((st - 8) // GT + 1))
                    transposes(bT, ctok[:, t % 2, :]).then_inc(s["tc"], 1)
                if has(st - 1):
                    values(st - 1, 0)
                    values(st - 1, 1)
                    probs_T(st - 1, 2)
                    probs_T(st - 1, 3)
                if has(st - 3):
                    t = st - 3
                    pe.wait_ge(s["hn"], t + 1)
                    pe.wait_ge(s["cl"], min(TILES, st - 1))
                    if t >= 1:
                        pe.wait_ge(s["lgd"], t)
                    transposes(bT, rows[:, (t // GT) % 2, t % GT, 0:D]).then_inc(s["th"], 1)
                if has(st - 2):
                    t = st - 2
                    pe.wait_ge(s["cl"], t + 1)
                    if t >= 1:
                        pe.wait_ge(s["x2d"], t)
                    if t == 0:
                        pe.wait_ge(s["wo_lo"], 1)
                    three(bO[:, :], lambda h, c: cT[:, h, c * P:(c + 1) * P], lambda h, c: wo_s[:, h, c, :], C).then_inc(s["op"], 1)
                if has(st - 1):
                    values(st - 1, 2)
                    values(st - 1, 3)
                if has(st - 3):
                    t = st - 3
                    pe.wait_ge(s["h2"], t + 1)
                    for c in range(C):
                        r = te.matmul(bT[:, 0:E], h2T[:, c * P:(c + 1) * P], gw_s[:, c, :], start=(c == 0), stop=(c == C - 1))
                    r.then_inc(s["rt"], 1)
                gr = (st - 7) // GT
                if (st - 7) % GT == 0 and 0 <= gr < GROUPS:
                    pe.wait_ge(s["hot_d"], 3 * gr + 1)
                    if has(st - 3):
                        pe.wait_ge(s["lgd"], st - 2)
                    rk = bT[:, 0:(GT + 1) * E].rearrange("p (t e) -> p t e", e=E)
                    te.matmul(rk, tri[:, :], picked[:, :, :], start=True, stop=False)
                    for j in range(GT):
                        r = te.matmul(rk[:, j + 1:GT + 1, :], ones[:, :],
                                      picked[:, j:j + 1, :].broadcast_to([P, GT - j, E]), start=False, stop=(j == GT - 1))
                    r.then_inc(s["rank"], 1)

            pe.wait_ge(s["counts"], 1)

            def rows_T(t):
                pe.wait_ge(s["rw"], 16 * t + 16)
                if not isinstance(t, int) or t > 0:
                    pe.wait_ge(s["rxl"], t)
                transposes(bQ, rowb[:, 0:D]).then_inc(s["tx2"], 1)

            def half(t, w, u):
                cs = slice(u * FF, (u + 1) * FF)
                return three(bS[u][:, :], lambda h, c: rT[:, h, c * P:(c + 1) * P], lambda h, c: w_gu[w][h][:, c, cs], C)

            def gates(t, w):
                pe.wait_ge(s["rxl"], t + 1)
                if not isinstance(t, int) or t > 0:
                    pe.wait_ge(s["sgd"], t)
                half(t, w, 0).then_inc(s["gt"], 1)

            def hidden_T(p):
                pe.wait_ge(s["hm"], p + 1)
                if not isinstance(p, int) or p > 0:
                    pe.wait_ge(s["hl"], p)
                transposes(bT, hid).then_inc(s["th2"], 1)

            def ups(t, w):
                half(t, w, 1).then_inc(s["up"], 1)

            def down(p, w):
                pe.wait_ge(s["hl"], p + 1)
                if not isinstance(p, int) or p > 0:
                    pe.wait_ge(s["accd"], p)
                three(bO[:, :], lambda h, c: hT[:, h, c * P:(c + 1) * P], lambda h, c: w_dn[w][h][:, c, :], C).then_inc(s["dnp"], 1)

            rows_T(0)
            for e in range(E):
                w = e % 2
                cnt = pe.value_load(ntile[0:1, e:e + 1], min_val=MINT, max_val=B * S // P)
                before = pe.value_load(tbase[0:1, e:e + 1], min_val=0, max_val=MAXT) if e else -1
                pe.wait_ge(s["wlo"], WCH * (e + 1))
                for k in range(2):
                    p = before + k
                    gates(p + 1, w)
                    if e or k:
                        hidden_T(p)
                    ups(p + 1, w)
                    rows_T(p + 2)
                    if e or k:
                        down(p, w if k else 1 - w)
                with pe.Fori(1, cnt - 1) as k:
                    p = before + 1 + k
                    gates(p + 1, w)
                    hidden_T(p)
                    ups(p + 1, w)
                    rows_T(p + 2)
                    down(p, w)
            last = pe.value_load(tbase[0:1, E:E + 1], min_val=0, max_val=MAXT)
            hidden_T(last)
            down(last, (E - 1) % 2)


_INS = ["x", "ctxT", "mask", "wq", "q_b", "wk", "k_b", "wv", "v_b", "wo", "o_b", "gw", "gu", "dn"]


def kernel(x, ctx_1024, mask_SxS2_bk1, L0_xattn_q_w, L0_xattn_q_b, L0_xattn_k_w, L0_xattn_k_b,
           L0_xattn_v_w, L0_xattn_v_b, L0_xattn_o_w, L0_xattn_o_b, L0_ffn_gate_w, L0_ffn_gate_up_proj,
           L0_ffn_down_proj):
    import numpy as np
    import concourse.bacc as bacc
    from concourse.bass_utils import run_bass_kernel_spmd

    def rows_first(a):
        a = np.asarray(a)
        return np.ascontiguousarray(a.reshape(-1, P, a.shape[1]).transpose(1, 0, 2))

    def by_head_group(b):
        return np.ascontiguousarray(np.asarray(b).reshape(J, P).T)

    def turned(w):
        return rows_first(np.asarray(w).T)

    given = {
        "x": x, "ctxT": np.stack([turned(c) for c in np.asarray(ctx_1024)]),
        "mask": rows_first(mask_SxS2_bk1),
        "wq": turned(L0_xattn_q_w), "q_b": by_head_group(L0_xattn_q_b),
        "wk": turned(L0_xattn_k_w), "k_b": by_head_group(L0_xattn_k_b),
        "wv": turned(L0_xattn_v_w), "v_b": L0_xattn_v_b, "wo": turned(L0_xattn_o_w), "o_b": L0_xattn_o_b,
        "gw": turned(L0_ffn_gate_w), "gu": L0_ffn_gate_up_proj, "dn": L0_ffn_down_proj,
    }
    nc = bacc.Bacc("TRN2", target_bir_lowering=False, num_devices=1)
    arrays, args = {}, []
    for name in _INS:
        a = np.ascontiguousarray(given[name])
        arrays[f"in_{name}"] = a
        args.append(nc.dram_tensor(f"in_{name}", a.shape, mybir.dt.from_np(a.dtype), kind="ExternalInput").ap())
    args.append(nc.dram_tensor("out_0", (B, S, D), F32, kind="ExternalOutput").ap())
    build(nc, *args)
    r = run_bass_kernel_spmd(nc, [arrays], core_ids=[0])
    return r.results[0]["out_0"]
```

```python
from contextlib import ExitStack

import concourse.bass as bass
from concourse import mybir

P = 128
F32 = mybir.dt.float32
F32R = mybir.dt.float32r
BF16 = mybir.dt.bfloat16
I32 = mybir.dt.int32
U32 = mybir.dt.uint32
U8 = mybir.dt.uint8
ALU = mybir.AluOpType
ACT = mybir.ActivationFunctionType
AX = mybir.AxisListType

B, S, D = 2, 2048, 512
KEYS, HEADS, HD = 77, 16, 32
KP = KEYS + 1
E, FF = 8, 512
LN_EPS, TOPK_EPS = 1e-5, 1e-9
C = D // P
HG = P // HD
J = HEADS // HG
GK = HG * KP
M = 3
MK = GK // M
VC = P + HG
TILES = B * S // P
GT = 4
GROUPS = TILES // GT
ROW = D + 1 + E
MINT = 3
REG = B * S + MINT * P
NOBODY = 8191
WCH = 6
MAXT = 2 * TILES + MINT * E
SCALE = 1.0 / float(HD) ** 0.5
MASKED = -1e30
assert GK % M == 0 and GK % 2 == 0


def build(nc, x, ctxT, mask, wq, q_b, wk, k_b, wv, v_b, wo, o_b, gw, gu, dn, out):
    with ExitStack() as ctx:
        def sb(name, shape, dt=F32):
            return ctx.enter_context(nc.sbuf_tensor(name, shape, dt))

        def sem(name):
            return ctx.enter_context(nc.semaphore(name))

        slots = nc.dram_tensor("slots", [E * REG, ROW], F32, kind="Internal").ap()
        xr_rows = x.rearrange("b s d -> (b s) d")
        out_rows = out.rearrange("b s d -> (b s) d")

        WE = C * (2 * FF) + C * D
        ops = sb("ops", [P, 4 * WE], F32R)
        CD = C * GT * P

        def part(at, inner):
            v = ops[:, at:at + 2 * CD].rearrange("p (h c n) -> p h c n", h=2, c=C)
            assert v.shape[3] == inner
            return v

        xT = [part(q * 2 * CD, 512) for q in range(2)]
        wq_s = part(4 * CD, D)
        qT = [part(6 * CD + q * 2 * CD, 512) for q in range(2)]
        wo_s = part(10 * CD, D)
        w_gu = [[ops[:, (2 * w + h) * WE:(2 * w + h) * WE + C * 2 * FF].rearrange("p (c n) -> p c n", c=C)
                 for h in range(2)] for w in range(2)]
        w_dn = [[ops[:, (2 * w + h) * WE + C * 2 * FF:(2 * w + h + 1) * WE].rearrange("p (c n) -> p c n", c=C)
                 for h in range(2)] for w in range(2)]
        kbd = sb("kbd", [P, 2 * B * J * GK], F32R)[:, :].rearrange("p (h b j n) -> p h b j n", h=2, b=B, j=J)
        kflat = kbd.rearrange("p h b j n -> p (h b j n)")
        vbd = sb("vbd", [P, 2 * B * J * M * VC], F32R)[:, :].rearrange(
            "p (h b j m n) -> p h b j m n", h=2, b=B, j=J, m=M)
        pT = sb("pT", [P, 2, 2, M * P], F32R)
        cT = sb("cT", [P, 2, C * P], F32R)
        rT = kflat[:, 0:2 * D].rearrange("p (h n) -> p h n", h=2)
        hT = cT

        stage = sb("stage", [P, WCH * 1024])
        xin = stage[:, 0:4 * D].rearrange("p (t n) -> p t n", t=4)
        SMW = HEADS * KP
        smx = stage[:, 4 * D:4 * D + 2 * SMW].rearrange("p (t n) -> p t n", t=2)
        c_at = 4 * D + 2 * SMW
        ctok = stage[:, c_at:c_at + 2 * D].rearrange("p (t n) -> p t n", t=2)
        h2T = stage[:, c_at + 2 * D:c_at + 3 * D]
        wraw = stage[:, :].rearrange("p (w n) -> p w n", w=WCH)
        xres = sb("xres", [P, 2, D])
        x2 = sb("x2", [P, 2, D])
        rows = sb("rows", [P, 2, GT, ROW])
        rflat = rows[:, :, :, :].rearrange("p q t n -> p (q t n)")
        mbias = sb("mbias", [P, S // P, KP], BF16)
        mraw = xres[:, 0, :].bitcast(U8)[:, 0:S // P * KP].rearrange("p (t n) -> p t n", n=KP)
        ident = sb("ident", [P, P])
        tri = sb("tri", [P, P], BF16)
        ones = sb("ones", [P, P], BF16)
        gw_s = sb("gw_s", [P, C, E])
        qb_s = sb("qb_s", [P, J])
        kb_s = sb("kb_s", [P, J])
        vb_s = x2[0:1, 1, :]
        ones1 = x2[0:1, 0, 2 * P:3 * P]
        ob_s = sb("ob_s", [P, D])
        hsel = sb("hsel", [P, M, HG])
        toki = sb("toki", [P, TILES], U32)
        iota8i = sb("iota8i", [P, E], I32)
        iota8 = sb("iota8", [P, E])
        firsti = sb("firsti", [P, E], I32)
        first = sb("first", [P, E])
        mhalf = sb("mhalf", [P, 1])
        st1, mv1, ve1, rs1, nm1 = (sb(n, [P, 4, w]) for n, w in
                                   (("st1", 6), ("mv1", 2), ("ve1", 1), ("rs1", 1), ("nm1", 1)))
        st2, mv2, ve2, rs2, nm2 = (sb(n, [P, 4, w]) for n, w in
                                   (("st2", 6), ("mv2", 2), ("ve2", 1), ("rs2", 1), ("nm2", 1)))
        mxs = sb("mxs", [P, 2, HEADS])
        rden = sb("rden", [P, 2, 2, HG])
        lg = sb("lg", [P, 2, GT, E])
        top = sb("top", [P, GT, E])
        topi = sb("topi", [P, GT, E], U32)
        topf = sb("topf", [P, GT, 2])
        hot = sb("hot", [P, 2, GT, E])
        picked = sb("picked", [P, GT + 1, E], BF16)
        dif = sb("dif", [P, GT, E])
        ex = sb("ex", [P, GT, E])
        zs = sb("zs", [P, GT, 1])
        rz = sb("rz", [P, GT, 1])
        pp = sb("pp", [P, GT, 2])
        rank = sb("rank", [P, GT + 1, E])
        count = sb("count", [P, E])
        slot = sb("slot", [P, GT, E])
        tmp = sb("tmp", [P, 2, GT, E])
        slotf = sb("slotf", [P, 2, GT])
        sloti = sb("sloti", [P, 2, 2, GT], U32)
        ntok = sb("ntok", [P, E], I32)
        ntile = sb("ntile", [P, E], I32)
        tbase = sb("tbase", [P, E + 1], I32)
        emptyrow = rflat[:, 0:ROW]
        padrow = rflat[:, ROW:2 * ROW]
        rowb = rflat[:, 0:ROW]
        sg = xres[:, 0, :]
        hid = xres[:, 1, :]
        acc = x2[:, 1, :]
        meta = [sb(f"meta{n}", [P, 1 + E], U32) for n in range(3)]
        zero = sb("zero", [P, 1 + E], U32)
        idle = sb("idle", [P, 1], U32)

        bT, bQ, bS0, bS1, bP0, bP1, bV, bO = (
            ctx.enter_context(nc.psum_tensor(n, [P, 512], F32))
            for n in ("bT", "bQ", "bS0", "bS1", "bP0", "bP1", "bV", "bO"))
        bS, bP = [bS0, bS1], [bP0, bP1]
        LOGITS = bO[:, 0:E]
        RANK = bO[:, E:E + (GT + 1) * E].rearrange("p (t e) -> p t e", e=E)

        names = """ld_wq ld_wo ld_wk ld_wv ld_ctx ld_mask ld_small mraw_set ctx_pad consts const_tiles
        cr_done wq_hi wq_lo wo_hi wo_lo kp kp_out kz k_hi k_lo vp v_tmp v_hi v_lo v_ones mask_done tok_done
        ln1 rs1d nm1d xn tx xh xl qp qh ql sp ma mxd sub ex_done pt ph pl pv rc cn tc ch cl op
        xb x2d ln2 rs2d nm2d hn th h2 rt lgd route dif_d exr hot_d rank prow pre_pads rank_d
        counts pads zrow cchain
        rw whi wlo gt sgd th2 hh hl up hm tx2 rxh rxl dnp gat accd sct mshift m0""".split()
        s = {n: sem(n) for n in names}
        x_in = [sem(f"x_in{i}") for i in range(4)]
        xr_in = [sem(f"xr_in{i}") for i in range(2)]
        x_st = [sem(f"x_st{i}") for i in range(2)]
        scat = [sem(f"scat{i}") for i in range(GT)]
        w_in = [sem(f"w_in{i}") for i in range(WCH)]

        def rows_of(g, i):
            return (i // 2) * S + (2 * g + i % 2) * P

        block = ctx.enter_context(nc.Block())

        W0_STEP = TILES - GT

        def w_slot(e, ch):
            return ch if e else ch % 2

        def w_loads(e, ch):
            if e == 0:
                return ch // 2 + 1
            return e + (WCH // 2 if ch < 2 else 0)

        def n_before(e, ch):
            if e == 0:
                return max(0, ch - 1)
            if e == 1:
                return ch + WCH - 1 if ch < 2 else 0
            return WCH * (e - 1) + ch + 1

        def load_w(eng, e, ch):
            at = w_slot(e, ch)
            if n_before(e, ch):
                eng.wait_ge(s["wlo"], n_before(e, ch))
            if ch < 4:
                eng.dma_start(wraw[:, at, :], gu[e, ch * P:(ch + 1) * P, :]).then_inc(w_in[at], 16)
            else:
                eng.dma_start(wraw[:, at, :].rearrange("p (c n) -> p c n", c=2),
                              dn[e].rearrange("(c p) n -> p c n", p=P)[:, 2 * (ch - 4):2 * (ch - 4) + 2, :]).then_inc(w_in[at], 16)

        def has(t):
            return 0 <= t < TILES

        ROUTE_STEPS = 2 * GT + 20
        STEPS = range(-9, TILES + 10)

        @block.sync
        def _(sp):
            sp.dma_start(stage[:, 0:4 * D].rearrange("p (c n) -> p c n", c=C),
                         wq).then_inc(s["ld_wq"], 16)
            sp.dma_start(stage[:, 4 * D:8 * D].rearrange("p (c n) -> p c n", c=C),
                         wo).then_inc(s["ld_wo"], 16)
            sp.dma_start(stage[:, 8 * D:12 * D].rearrange("p (c n) -> p c n", c=C),
                         wk).then_inc(s["ld_wk"], 16)
            sp.dma_start(rflat[:, 0:4 * D].rearrange("p (c n) -> p c n", c=C),
                         wv).then_inc(s["ld_wv"], 16)

            def load_x(t):
                g, i = t // GT, t % GT
                if t >= 4:
                    sp.wait_ge(s["tx"], t - 3)
                elif i == 0:
                    sp.wait_ge(s["wq_hi"], 1)
                    sp.wait_ge(s["wq_lo"], 1)
                sp.dma_start(xin[:, i, :], xr_rows[bass.ds(rows_of(g, i), P), :]).then_inc(x_in[i], 16)

            for t in range(4):
                load_x(t)
            sp.wait_ge(s["prow"], 2)
            for e in range(E):
                sp.dma_start(slots[e * REG:e * REG + MINT * P, :].rearrange("(k p) n -> p k n", p=P),
                             emptyrow[:, None, :].broadcast_to([P, MINT, ROW])).then_inc(s["pre_pads"], 16)
            for st in STEPS:
                if 4 <= st + 12 < TILES:
                    load_x(st + 12)
                if has(st):
                    i = st % GT
                    if st >= 2:
                        sp.wait_ge(s["x2d"], st - 1)
                    elif st == 0:
                        sp.wait_ge(s["v_lo"], 2 * M)
                    sp.dma_start(xres[:, st % 2, :], xr_rows[bass.ds(rows_of(st // GT, i), P), :]).then_inc(xr_in[st % 2], 16)
                if has(st - 2):
                    t = st - 2
                    sp.wait_ge(s["x2d"], t + 1)
                    sp.dma_start(out_rows[bass.ds(rows_of(t // GT, t % GT), P), :], x2[:, t % 2, :]).then_inc(x_st[t % 2], 16)
                if st == W0_STEP - 1:
                    sp.wait_ge(s["tx"], TILES)
                    load_w(sp, 0, 0)
                    load_w(sp, 0, 1)
                if W0_STEP < st < W0_STEP + WCH - 1:
                    load_w(sp, 0, st - W0_STEP + 1)

            sp.wait_ge(s["pt"], TILES * J)
            sp.wait_ge(s["tc"], TILES)
            sp.wait_ge(s["rt"], TILES)
            for ch in range(WCH):
                load_w(sp, 1, ch)

            def pad(e):
                n = sp.value_load(ntok[0:1, e:e + 1], min_val=0, max_val=B * S)
                sp.dma_start(slots[bass.ds(n + e * REG, P), :], padrow).then_inc(s["pads"], 16)

            sp.wait_ge(s["counts"], 1)
            sp.wait_ge(s["prow"], 4)
            pad(0)
            sp.wait_ge(s["pads"], 16)
            for q in scat:
                sp.wait_ge(q, 16 * 2 * GROUPS)

            def load_rows(e, k, t):
                if not isinstance(t, int) or t > 0:
                    sp.wait_ge(s["tx2"], t)
                    sp.wait_ge(s["m0"], t)
                sp.dma_start(rowb, slots[bass.ds(k * P + e * REG, P), :]).then_inc(s["rw"], 16)

            for e in range(E):
                cnt = sp.value_load(ntile[0:1, e:e + 1], min_val=MINT, max_val=B * S // P)
                base = 1 + sp.value_load(tbase[0:1, e:e + 1], min_val=0, max_val=MAXT) if e else 0
                load_rows(e, 0, base)
                if e == 0:
                    for n in range(1, E):
                        pad(n)
                load_rows(e, 1, base + 1)
                if e == 0:
                    sp.wait_ge(s["pads"], 16 * E)
                with sp.Fori(2, cnt) as k:
                    load_rows(e, k, base + k)
            tend = 1 + sp.value_load(tbase[0:1, E:E + 1], min_val=0, max_val=MAXT)
            load_rows(0, 0, tend)

        @block.gpsimd
        def _(pool):
            g_ = nc.gpsimd
            pool.dma_start(gw_s[:, :, :], gw).then_inc(s["ld_small"], 16)
            pool.dma_start(qb_s[:, :], q_b).then_inc(s["ld_small"], 16)
            pool.dma_start(kb_s[:, :], k_b).then_inc(s["ld_small"], 16)
            pool.dma_start(vb_s[:, :], v_b[None, :]).then_inc(s["ld_small"], 16)
            pool.dma_start(ob_s[:, :], o_b[None, :].broadcast_to([P, D])).then_inc(s["ld_small"], 16)
            g_.memset(ident[:, :], 0.0).then_inc(s["consts"], 1)
            g_.memset(tri[:, :], 1.0).then_inc(s["consts"], 1)
            g_.memset(hsel[:, :, :], 1.0).then_inc(s["consts"], 1)
            g_.memset(ones[:, :], 1.0).then_inc(s["const_tiles"], 1)
            g_.memset(ones1[:, :], 1.0).then_inc(s["const_tiles"], 1)
            g_.memset(mhalf[:, :], -0.5).then_inc(s["const_tiles"], 1)
            pool.wait_ge(s["consts"], 3)
            g_.affine_select(out=ident[:, :], in_=ident[:, :], compare_op=ALU.not_equal, fill=1.0, base=0,
                             pattern=[[-1, P]], channel_multiplier=1).then_inc(s["const_tiles"], 1)
            g_.affine_select(out=tri[:, :], in_=tri[:, :], compare_op=ALU.is_gt, fill=0.0, base=0,
                             pattern=[[1, P]], channel_multiplier=-1).then_inc(s["const_tiles"], 1)
            g_.affine_select(out=hsel[:, :, :], in_=hsel[:, :, :], compare_op=ALU.is_ge, fill=0.0, base=0,
                             pattern=[[MK, M], [-KP, HG]], channel_multiplier=1).then_inc(s["consts"], 1)
            pool.wait_ge(s["consts"], 4)
            g_.affine_select(out=hsel[:, :, :], in_=hsel[:, :, :], compare_op=ALU.is_ge, fill=0.0, base=KP - 1,
                             pattern=[[-MK, M], [KP, HG]], channel_multiplier=-1).then_inc(s["const_tiles"], 1)
            g_.iota(toki[:, :], pattern=[[2 * P, GROUPS], [S, 2], [P, 2]], base=0, channel_multiplier=1).then_inc(s["tok_done"], 1)
            g_.iota(iota8i[:, :], pattern=[[1, E]], base=0, channel_multiplier=0).then_inc(s["tok_done"], 1)
            g_.iota(firsti[:, :], pattern=[[REG, E]], base=0, channel_multiplier=0).then_inc(s["tok_done"], 1)
            g_.memset(picked[:, GT, :], 0.0).then_inc(s["const_tiles"], 1)

            def rstd(t, ve, rs, mv, nm, from_, rsd, nmd, per):
                i = t % 4
                pool.wait_ge(s[from_], per * t + per)
                g_.tensor_tensor(rs[:, i, :], ve[:, i, :], mhalf[:, :], ALU.pow).then_inc(s[rsd], 1)
                pool.wait_ge(s[rsd], t + 1)
                g_.tensor_scalar(nm[:, i, :], mv[:, i, 0:1], rs[:, i, 0:1], -1.0, ALU.mult, ALU.mult).then_inc(s[nmd], 1)

            pool.wait_ge(s["vp"], B * M)
            g_.memset(emptyrow, 0.0).then_inc(s["prow"], 1)
            pool.wait_ge(s["prow"], 1)
            g_.memset(emptyrow[:, D:D + 1].bitcast(U32), NOBODY).then_inc(s["prow"], 1)
            for st in STEPS:
                if has(st - 3):
                    rstd(st - 3, ve2, rs2, mv2, nm2, "ln2", "rs2d", "nm2d", 3)
                if st == TILES + 5:
                    pool.wait_ge(scat[1], 16 * 2 * (GROUPS - 1))
                    g_.memset(padrow, 0.0).then_inc(s["prow"], 1)
                    pool.wait_ge(s["prow"], 3)
                    g_.memset(padrow[:, D:D + 1].bitcast(U32), NOBODY).then_inc(s["prow"], 1)
                if has(st - 10):
                    gs, i = (st - 10) // GT, (st - 10) % GT
                    if i == 0:
                        pool.wait_ge(s["route"], ROUTE_STEPS * (gs + 1))
                    if st == 10:
                        pool.wait_ge(s["pre_pads"], 16 * E)
                    if gs:
                        pool.wait_ge(scat[i], 16 * 2 * gs)
                    for k in range(2):
                        pool.indirect_dma_start(
                            out=slots[:, :], out_offset=bass.IndirectOffsetOnAxis(ap=sloti[:, gs % 2, k, i:i + 1], axis=0),
                            in_=rows[:, gs % 2, i, :], in_offset=None).then_inc(scat[i], 16)
                if has(st - 1):
                    t = st - 1
                    if t == 0:
                        pool.wait_ge(s["ld_small"], 16 * 5)
                    pool.wait_ge(xr_in[t % 2], 16 * (t // 2 + 1))
                    g_.tensor_tensor(xres[:, t % 2, :], xres[:, t % 2, :], ob_s[:, :], ALU.add).then_inc(s["xb"], 1)
                if has(st + 9):
                    if st + 9 == 0:
                        pool.wait_ge(s["const_tiles"], 3)
                    rstd(st + 9, ve1, rs1, mv1, nm1, "ln1", "rs1d", "nm1d", 3)
                if has(st):
                    pool.wait_ge(s["mxd"], st + 1)
                    v = smx[:, st % 2, :].rearrange("p (h n) -> p h n", h=HEADS)
                    g_.tensor_tensor(v, v, mxs[:, st % 2, :, None].broadcast_to([P, HEADS, KP]),
                                     ALU.subtract).then_inc(s["sub"], 1)

            for q in x_st:
                pool.wait_ge(q, 16 * TILES // 2)

            def idle_add():
                g_.tensor_tensor(idle[:, :], zero[:, 0:1], zero[:, 0:1], ALU.add)

            def combine(t):
                pool.wait_ge(s["accd"], t + 1)
                idle_add()
                pool.indirect_dma_start(
                    out=out_rows[:, :], out_offset=bass.IndirectOffsetOnAxis(ap=meta[2][:, 0:1], axis=0),
                    in_=acc, in_offset=None, compute_op=ALU.add,
                    bounds_check=B * S - 1, oob_is_err=False).then_inc(s["sct"], 16)
                pool.wait_ge(s["sct"], 16 * t + 16)

            def move(to, of):
                return g_.tensor_tensor(meta[to][:, :], meta[of][:, :], zero[:, :], ALU.add)

            def shift(t):
                pool.wait_ge(s["m0"], t + 2)
                move(2, 1).then_inc(s["mshift"], 1)
                pool.wait_ge(s["mshift"], 2 * t + 1)
                move(1, 0).then_inc(s["mshift"], 1)

            pool.wait_ge(s["m0"], 1)
            g_.memset(zero[:, :], 0).then_inc(s["zrow"], 1)
            pool.wait_ge(s["zrow"], 1)
            move(1, 0).then_inc(s["zrow"], 1)
            pool.wait_ge(s["counts"], 1)
            for e in range(E):
                cnt = pool.value_load(ntile[0:1, e:e + 1], min_val=MINT, max_val=B * S // P)
                base = 1 + pool.value_load(tbase[0:1, e:e + 1], min_val=0, max_val=MAXT) if e else 0
                with pool.Fori(0, cnt) as k:
                    shift(base + k)
                    combine(base + k)
            tend = 1 + pool.value_load(tbase[0:1, E:E + 1], min_val=0, max_val=MAXT)
            pool.wait_ge(s["sct"], 16 * tend)

        @block.scalar
        def _(act):
            a = nc.scalar

            def copy(o, i):
                return a.activation(o, i, ACT.Copy)

            cx = rflat[:, 4 * D:4 * D + C * B * KP].rearrange("p (c b n) -> p c b n", c=C, b=B)
            def ph(t, j):
                n = 4 * t + j
                act.wait_ge(s["pt"], n + 1)
                if n >= 2:
                    act.wait_ge(s["pv"], n - 1)
                copy(pT[0:MK, j % 2, 0, :], bP[j % 2][0:MK, 0:M * P]).then_inc(s["ph"], 1)

            act.wait_ge(s["ctx_pad"], 1)
            for b in range(B):
                act.dma_start(cx[:, :, b, 0:KEYS], ctxT[b]).then_inc(s["ld_ctx"], 16)
            act.wait_ge(s["mraw_set"], 1)
            act.dma_start(mraw[:, :, 0:KEYS], mask).then_inc(s["ld_mask"], 16)
            act.wait_ge(s["ld_wq"], 16)
            copy(wq_s[:, 0].rearrange("p c n -> p (c n)"), stage[:, 0:4 * D]).then_inc(s["wq_hi"], 1)
            act.wait_ge(s["ld_wo"], 16)
            copy(wo_s[:, 0].rearrange("p c n -> p (c n)"), stage[:, 4 * D:8 * D]).then_inc(s["wo_hi"], 1)
            act.wait_ge(s["ld_small"], 16 * 5)
            ktmp = x2[:, 0, 0:B * KEYS].rearrange("p (b n) -> p b n", b=B)
            for j in range(J):
                act.wait_ge(s["kp"], j + 1)
                if j >= 1:
                    act.wait_ge(s["k_lo"], HG * j)
                a.activation(ktmp, bP[0][:, 0:B * KEYS].rearrange("p (b n) -> p b n", b=B), ACT.Identity,
                             bias=kb_s[:, j:j + 1]).then_inc(s["kp_out"], 1)
                act.wait_ge(s["kp_out"], j + 1)
                if j == 0:
                    act.wait_ge(s["kz"], 1)
                for h in range(HG):
                    rs = slice(h * HD, (h + 1) * HD)
                    copy(kbd[rs, 0, :, j, h * KP:h * KP + KEYS], ktmp[rs]).then_inc(s["k_hi"], 1)
            for n in range(B * M):
                b, m = n // M, n % M
                act.wait_ge(s["v_tmp"], n + 1)
                vt = xres[0:MK, n % 2, :].rearrange("p (j n) -> p j n", j=J)
                copy(vbd[0:MK, 0, b, :, m, 0:P], vt).then_inc(s["v_hi"], 1)

            def split_hi(e, ch):
                act.wait_ge(w_in[w_slot(e, ch)], 16 * w_loads(e, ch))
                w = e % 2
                dst = (w_gu[w][0][:, ch, :] if ch < 4 else
                       w_dn[w][0][:, 2 * (ch - 4):2 * (ch - 4) + 2, :].rearrange("p c n -> p (c n)"))
                copy(dst, wraw[:, w_slot(e, ch), :]).then_inc(s["whi"], 1)

            def norm(t, dst, src, rs, nm):
                i = t % 4
                return a.activation(dst, src, ACT.Identity, scale=rs[:, i, 0:1], bias=nm[:, i, 0:1])

            for st in STEPS:
                g, i = st // GT, st % GT
                if has(st - 1):
                    ph(st - 1, 0)
                if has(st + 8):
                    t = st + 8
                    act.wait_ge(s["tx"], t + 1)
                    if t >= 8 and t % GT == 0:
                        act.wait_ge(s["qp"], 4 * (t // GT - 1))
                    copy(xT[(t // GT) % 2][:, 0, :, (t % GT) * P:(t % GT + 1) * P],
                         bT[:, :].rearrange("p (c n) -> p c n", c=C)).then_inc(s["xh"], 1)
                if has(st - 1):
                    ph(st - 1, 1)
                gq = g + 1
                if 0 <= gq < GROUPS:
                    act.wait_ge(s["qp"], 4 * gq + i + 1)
                    if gq >= 2 and i == 0:
                        act.wait_ge(s["sp"], 16 * (gq - 1))
                    a.activation(qT[gq % 2][:, 0, i, :], bQ[:, :], ACT.Identity,
                                 bias=qb_s[:, i:i + 1]).then_inc(s["qh"], 1)
                if has(st - 3):
                    t = st - 3
                    act.wait_ge(s["nm2d"], t + 1)
                    act.wait_ge(s["x2d"], t + 1)
                    if t == 0:
                        act.wait_ge(s["pre_pads"], 16 * E)
                    if t >= 2 * GT:
                        act.wait_ge(scat[t % GT], 16 * 2 * (t // GT - 1))
                    norm(t, rows[:, (t // GT) % 2, t % GT, 0:D], x2[:, t % 2, :], rs2, nm2).then_inc(s["hn"], 1)
                if has(st - 2):
                    t = st - 2
                    act.wait_ge(s["tc"], t + 1)
                    if t >= 1:
                        act.wait_ge(s["op"], t)
                    copy(cT[:, 0, :], bT[:, :]).then_inc(s["ch"], 1)
                if has(st - 1):
                    ph(st - 1, 2)
                    ph(st - 1, 3)
                if has(st):
                    act.wait_ge(s["sub"], st + 1)
                    a.activation(smx[:, st % 2, :], smx[:, st % 2, :], ACT.Exp, scale=SCALE).then_inc(s["ex_done"], 1)
                if has(st - 3):
                    act.wait_ge(s["th"], st - 2)
                    if st - 3 >= 1:
                        act.wait_ge(s["rt"], st - 3)
                    copy(h2T, bT[:, :]).then_inc(s["h2"], 1)
                if has(st + 9):
                    t = st + 9
                    act.wait_ge(s["nm1d"], t + 1)
                    norm(t, xin[:, t % 4, :], xin[:, t % 4, :], rs1, nm1).then_inc(s["xn"], 1)
                if 0 <= st - W0_STEP < WCH:
                    if st == W0_STEP:
                        act.wait_ge(s["qp"], 4 * GROUPS)
                    split_hi(0, st - W0_STEP)
                gr = (st - 7) // GT
                if (st - 7) % GT == 0 and 0 <= gr < GROUPS:
                    act.wait_ge(s["dif_d"], gr + 1)
                    a.activation(ex[:, :, :], dif[:, :, :], ACT.Exp).then_inc(s["exr"], 1)

            act.wait_ge(s["op"], TILES)
            act.wait_ge(s["counts"], 1)

            def silu(t):
                act.wait_ge(s["gt"], t + 1)
                if not isinstance(t, int) or t > 0:
                    act.wait_ge(s["hm"], t)
                a.activation(sg, bS0[:, :], ACT.Silu).then_inc(s["sgd"], 1)

            def hidden_hi(p):
                act.wait_ge(s["th2"], p + 1)
                if not isinstance(p, int) or p > 0:
                    act.wait_ge(s["dnp"], p)
                copy(hT[:, 0, :], bT[:, :]).then_inc(s["hh"], 1)

            def rows_hi(t):
                act.wait_ge(s["tx2"], t + 1)
                if not isinstance(t, int) or t > 0:
                    act.wait_ge(s["up"], t)
                copy(rT[:, 0, :], bQ[:, :]).then_inc(s["rxh"], 1)

            rows_hi(0)
            for e in range(E):
                cnt = act.value_load(ntile[0:1, e:e + 1], min_val=MINT, max_val=B * S // P)
                before = act.value_load(tbase[0:1, e:e + 1], min_val=0, max_val=MAXT) if e else -1
                for k in range(2):
                    p = before + k
                    silu(p + 1)
                    if e or k:
                        hidden_hi(p)
                    if e + 1 < E:
                        if k == 0 and e:
                            act.wait_ge(s["up"], p + 1)
                        split_hi(e + 1, 3 * k)
                    rows_hi(p + 2)
                    if e + 1 < E:
                        if k == 1 and e:
                            act.wait_ge(s["dnp"], p)
                        split_hi(e + 1, 3 * k + 1)
                        split_hi(e + 1, 3 * k + 2)
                if e + 2 < E:
                    for ch in range(WCH):
                        load_w(act, e + 2, ch)
                with act.Fori(1, cnt - 1) as k:
                    p = before + 1 + k
                    silu(p + 1)
                    hidden_hi(p)
                    rows_hi(p + 2)
            last = act.value_load(tbase[0:1, E:E + 1], min_val=0, max_val=MAXT)
            hidden_hi(last)

        @block.vector
        def _(dve):
            v = nc.vector

            def f(ap):
                return ap.bitcast(F32)

            def lo(dst, full, hi):
                return v.tensor_tensor(dst, full, f(hi), ALU.subtract)

            cx = rflat[:, 4 * D:4 * D + C * B * KP].rearrange("p (c b n) -> p c b n", c=C, b=B)
            cr = rflat[:, 4 * D + C * B * KP:4 * D + C * B * KP + C * GK].rearrange("p (c h n) -> p c h n", c=C, h=HG)
            v.memset(rflat[:, 4 * D:4 * D + C * B * KP], 0.0).then_inc(s["ctx_pad"], 1)
            v.memset(mraw[:, :, :], 1).then_inc(s["mraw_set"], 1)
            v.memset(f(kflat), 0.0).then_inc(s["kz"], 1)
            v.memset(f(vbd[:, 1, :, :, :, :].rearrange("p b j m n -> p (b j m n)")), 0.0).then_inc(s["kz"], 1)
            dve.wait_ge(s["wq_hi"], 1)
            lo(wq_s[:, 1].rearrange("p c n -> p (c n)"), stage[:, 0:4 * D],
               wq_s[:, 0].rearrange("p c n -> p (c n)")).then_inc(s["wq_lo"], 1)
            dve.wait_ge(s["tok_done"], 3)
            v.tensor_copy(iota8[:, :], iota8i[:, :]).then_inc(s["tok_done"], 1)
            v.tensor_copy(count[:, :], firsti[:, :]).then_inc(s["tok_done"], 1)
            v.tensor_copy(first[:, :], firsti[:, :]).then_inc(s["tok_done"], 1)
            dve.wait_ge(s["ld_mask"], 16)
            v.tensor_scalar(mbias[:, :, :], mraw[:, :, :], MASKED, None, ALU.mult).then_inc(s["mask_done"], 1)

            def ln(t, src, stt, mv, ve, name):
                i = t % 4
                v.bn_stats(stt[:, i, :], src).then_inc(s[name], 1)
                dve.wait_ge(s[name], 3 * t + 1)
                v.bn_aggr(mv[:, i, :], stt[:, i, :]).then_inc(s[name], 1)
                dve.wait_ge(s[name], 3 * t + 2)
                v.tensor_scalar(ve[:, i, :], mv[:, i, 1:2], LN_EPS, None, ALU.add).then_inc(s[name], 1)

            def ln_x(t):
                dve.wait_ge(x_in[t % 4], 16 * (t // 4 + 1))
                ln(t, xin[:, t % 4, :], st1, mv1, ve1, "ln1")

            dve.wait_ge(s["ld_ctx"], 16 * B)
            for b in range(B):
                if b:
                    dve.wait_ge(s["vp"], M * b)
                for c in range(C):
                    r = v.tensor_copy(cr[:, c], cx[:, c, b, None, :].broadcast_to([P, HG, KP]))
                r.then_inc(s["cr_done"], 1)
                if b == 0:
                    ktmp = x2[:, 0, 0:B * KEYS].rearrange("p (b n) -> p b n", b=B)
                    for j in range(J):
                        for h in range(HG):
                            rs = slice(h * HD, (h + 1) * HD)
                            dve.wait_ge(s["k_hi"], HG * j + h + 1)
                            lo(kbd[rs, 1, :, j, h * KP:h * KP + KEYS], ktmp[rs],
                               kbd[rs, 0, :, j, h * KP:h * KP + KEYS]).then_inc(s["k_lo"], 1)
                    dve.wait_ge(s["const_tiles"], 7)
                for m in range(M):
                    n = b * M + m
                    dve.wait_ge(s["vp"], n + 1)
                    vt = xres[0:MK, n % 2, :].rearrange("p (j n) -> p j n", j=J)
                    for j in range(J):
                        r = v.tensor_tensor(vt[:, j].rearrange("p (h n) -> p h n", h=HG),
                                            bP[n % 2][0:MK, j * P:(j + 1) * P].rearrange("p (h n) -> p h n", h=HG),
                                            hsel[0:MK, m, :, None].broadcast_to([MK, HG, HD]), ALU.mult)
                    r.then_inc(s["v_tmp"], 1)
                    v.tensor_copy(vbd[0:MK, 0, b, :, m, P:VC],
                                  hsel[0:MK, m, None, :].broadcast_to([MK, J, HG])).then_inc(s["v_ones"], 1)
                    dve.wait_ge(s["v_hi"], n + 1)
                    lo(vbd[0:MK, 1, b, :, m, 0:P], vt, vbd[0:MK, 0, b, :, m, 0:P]).then_inc(s["v_lo"], 1)
            dve.wait_ge(s["wo_hi"], 1)
            lo(wo_s[:, 1].rearrange("p c n -> p (c n)"), stage[:, 4 * D:8 * D],
               wo_s[:, 0].rearrange("p c n -> p (c n)")).then_inc(s["wo_lo"], 1)

            def pl(t, j):
                dve.wait_ge(s["ph"], 4 * t + j + 1)
                lo(pT[0:MK, j % 2, 1, :], bP[j % 2][0:MK, 0:M * P], pT[0:MK, j % 2, 0, :]).then_inc(s["pl"], 1)

            def mask_add(t, j):
                dve.wait_ge(s["sp"], 4 * t + j + 1)
                if t >= 2 and j == 0:
                    dve.wait_ge(s["pt"], 4 * (t - 1))
                if t == 0 and j == 0:
                    dve.wait_ge(s["wo_lo"], 1)
                    dve.wait_ge(s["kp"], J)
                g, i = t // GT, t % GT
                mt = 2 * g + i % 2
                v.tensor_tensor(smx[:, t % 2, j * GK:(j + 1) * GK].rearrange("p (h n) -> p h n", h=HG),
                                bS[j % 2][:, 0:GK].rearrange("p (h n) -> p h n", h=HG),
                                mbias[:, bass.ds(mt, 1), :].broadcast_to([P, HG, KP]), ALU.add).then_inc(s["ma"], 1)

            def context(t, h):
                dve.wait_ge(s["pv"], 4 * t + 2 * h + 2)
                pvv = bV[:, 0:2 * VC].rearrange("p (j n) -> p j n", j=2)
                v.reciprocal(rden[:, h], pvv[:, :, P:VC]).then_inc(s["rc"], 1)
                dve.wait_ge(s["rc"], 2 * t + h + 1)
                if t >= 2 and h == 0:
                    dve.wait_ge(s["tc"], t - 1)
                v.tensor_tensor(ctok[:, t % 2, h * 256:(h + 1) * 256].rearrange("p (j h n) -> p j h n", j=2, h=HG),
                                pvv[:, :, 0:P].rearrange("p j (h n) -> p j h n", h=HG),
                                rden[:, h, :, :, None].broadcast_to([P, 2, HG, HD]), ALU.mult).then_inc(s["cn"], 1)

            def split_lo(e, ch):
                dve.wait_ge(s["whi"], e * WCH + ch + 1)
                w = e % 2

                def at_(h):
                    return (w_gu[w][h][:, ch, :] if ch < 4 else
                            w_dn[w][h][:, 2 * (ch - 4):2 * (ch - 4) + 2, :].rearrange("p c n -> p (c n)"))
                lo(at_(1), wraw[:, w_slot(e, ch), :], at_(0)).then_inc(s["wlo"], 1)

            def route_choice(g):
                n = ROUTE_STEPS * g
                dve.wait_ge(s["lgd"], GT * (g + 1))
                for i in range(GT):
                    v.max(top[:, i, :], lg[:, g % 2, i, :]).then_inc(s["route"], 1)
                dve.wait_ge(s["route"], n + GT)
                for i in range(GT):
                    v.max_index(topi[:, i, :], top[:, i, :], lg[:, g % 2, i, :]).then_inc(s["route"], 1)
                v.tensor_tensor(dif[:, :, :], top[:, :, :], top[:, :, 0:1].broadcast_to([P, GT, E]),
                                ALU.subtract).then_inc(s["dif_d"], 1)
                dve.wait_ge(s["route"], n + 2 * GT)
                v.tensor_copy(topf[:, :, :], topi[:, :, 0:2]).then_inc(s["route"], 1)
                dve.wait_ge(s["route"], n + 2 * GT + 1)
                for k in range(2):
                    v.tensor_tensor(hot[:, k], iota8[:, None, :].broadcast_to([P, GT, E]),
                                    topf[:, :, k:k + 1].broadcast_to([P, GT, E]), ALU.is_equal).then_inc(s["route"], 1)
                dve.wait_ge(s["route"], n + 2 * GT + 3)
                v.tensor_tensor(picked[:, 0:GT, :], hot[:, 0], hot[:, 1], ALU.add).then_inc(s["hot_d"], 1)

            def route_weights(g):
                n = ROUTE_STEPS * g + 2 * GT + 3
                q = g % 2
                dve.wait_ge(s["exr"], g + 1)
                v.tensor_reduce(zs[:, :, 0], ex[:, :, :], AX.X, ALU.add).then_inc(s["route"], 1)
                dve.wait_ge(s["route"], n + 1)
                v.reciprocal(rz[:, :, 0], zs[:, :, 0]).then_inc(s["route"], 1)
                dve.wait_ge(s["route"], n + 2)
                v.tensor_tensor(pp[:, :, :], ex[:, :, 0:2], rz[:, :, :].broadcast_to([P, GT, 2]), ALU.mult).then_inc(s["route"], 1)
                for r in range(2):
                    dve.wait_ge(s["route"], n + 3 * r + 3)
                    v.scalar_tensor_tensor(zs[:, :, 0], pp[:, :, 0], TOPK_EPS, pp[:, :, 1], ALU.add, ALU.add).then_inc(s["route"], 1)
                    dve.wait_ge(s["route"], n + 3 * r + 4)
                    v.reciprocal(rz[:, :, 0], zs[:, :, 0]).then_inc(s["route"], 1)
                    dve.wait_ge(s["route"], n + 3 * r + 5)
                    v.tensor_tensor(pp[:, :, :], pp[:, :, :], rz[:, :, :].broadcast_to([P, GT, 2]), ALU.mult).then_inc(s["route"], 1)
                dve.wait_ge(s["route"], n + 9)
                for k in range(2):
                    v.tensor_tensor(tmp[:, k], hot[:, k], pp[:, :, k:k + 1].broadcast_to([P, GT, E]), ALU.mult).then_inc(s["route"], 1)
                v.tensor_copy(rows[:, q, :, D].bitcast(U32), toki[:, bass.ds(g * GT, GT)]).then_inc(s["route"], 1)
                dve.wait_ge(s["route"], n + 11)
                v.tensor_tensor(rows[:, q, :, D + 1:ROW], tmp[:, 0], tmp[:, 1], ALU.add).then_inc(s["route"], 1)

            def route_slots(g):
                n = ROUTE_STEPS * g + 2 * GT + 16
                dve.wait_ge(s["rank_d"], g + 1)
                v.tensor_tensor(slot[:, :, :], rank[:, 0:GT, :],
                                count[:, None, :].broadcast_to([P, GT, E]), ALU.add).then_inc(s["hot_d"], 1)
                dve.wait_ge(s["hot_d"], 3 * g + 2)
                v.tensor_tensor(count[:, :], count[:, :], rank[:, GT, :], ALU.add).then_inc(s["hot_d"], 1)
                dve.wait_ge(s["route"], n)
                for k in range(2):
                    v.tensor_tensor(tmp[:, k], slot[:, :, :], hot[:, k], ALU.mult).then_inc(s["route"], 1)
                dve.wait_ge(s["route"], n + 2)
                v.tensor_reduce(slotf[:, :, :], tmp[:, :, :, :], AX.X, ALU.add).then_inc(s["route"], 1)
                dve.wait_ge(s["route"], n + 3)
                v.tensor_copy(sloti[:, g % 2, :, :], slotf[:, :, :]).then_inc(s["route"], 1)

            for st in STEPS:
                g, i = st // GT, st % GT
                if has(st):
                    mask_add(st, 0)
                    mask_add(st, 1)
                if has(st - 1):
                    pl(st - 1, 0)
                if has(st + 8):
                    t = st + 8
                    dve.wait_ge(s["xh"], t + 1)
                    cs = slice((t % GT) * P, (t % GT + 1) * P)
                    lo(xT[(t // GT) % 2][:, 1, :, cs], bT[:, :].rearrange("p (c n) -> p c n", c=C),
                       xT[(t // GT) % 2][:, 0, :, cs]).then_inc(s["xl"], 1)
                if has(st):
                    mask_add(st, 2)
                if has(st - 1):
                    pl(st - 1, 1)
                if has(st):
                    mask_add(st, 3)
                    dve.wait_ge(s["ma"], 4 * st + 4)
                    v.tensor_reduce(mxs[:, st % 2, :], smx[:, st % 2, :].rearrange("p (h n) -> p h n", h=HEADS),
                                    AX.X, ALU.max).then_inc(s["mxd"], 1)
                if has(st + 9):
                    ln_x(st + 9)
                gq = g + 1
                if 0 <= gq < GROUPS:
                    dve.wait_ge(s["qh"], 4 * gq + i + 1)
                    v.scalar_tensor_tensor(qT[gq % 2][:, 1, i, :], bQ[:, :], qb_s[:, i:i + 1], f(qT[gq % 2][:, 0, i, :]),
                                           ALU.add, ALU.subtract).then_inc(s["ql"], 1)
                if has(st - 2):
                    dve.wait_ge(s["ch"], st - 1)
                    lo(cT[:, 1, :], bT[:, :], cT[:, 0, :]).then_inc(s["cl"], 1)
                if has(st - 1):
                    context(st - 1, 0)
                    pl(st - 1, 2)
                    pl(st - 1, 3)
                if (st - 7) % GT == 0 and has(st - 7):
                    route_choice((st - 7) // GT)
                if (st - 8) % GT == 0 and has(st - 8):
                    route_weights((st - 8) // GT)
                if (st - 9) % GT == 0 and has(st - 9):
                    route_slots((st - 9) // GT)
                if has(st - 2):
                    t = st - 2
                    dve.wait_ge(s["op"], t + 1)
                    dve.wait_ge(s["xb"], t + 1)
                    if t >= 2:
                        dve.wait_ge(x_st[t % 2], 16 * (t // 2))
                        dve.wait_ge(s["hn"], t - 1)
                    v.tensor_tensor(x2[:, t % 2, :], bO[:, :], xres[:, t % 2, :], ALU.add).then_inc(s["x2d"], 1)
                    dve.wait_ge(s["x2d"], t + 1)
                    ln(t, x2[:, t % 2, :], st2, mv2, ve2, "ln2")
                if has(st - 1):
                    context(st - 1, 1)
                if has(st - 3):
                    t = st - 3
                    dve.wait_ge(s["rt"], t + 1)
                    if (st - 7) % GT == 0 and has(st - 7):
                        dve.wait_ge(s["rank"], (st - 7) // GT + 1)
                    v.tensor_copy(lg[:, (t // GT) % 2, t % GT, :], LOGITS).then_inc(s["lgd"], 1)
                if (st - 7) % GT == 0 and has(st - 7):
                    dve.wait_ge(s["rank"], (st - 7) // GT + 1)
                    v.tensor_copy(rank[:, :, :], RANK).then_inc(s["rank_d"], 1)

                if 0 <= st - W0_STEP < WCH:
                    split_lo(0, st - W0_STEP)

            dve.wait_ge(s["hot_d"], 3 * GROUPS)
            v.tensor_tensor(ntok[:, :], count[:, :], first[:, :], ALU.subtract).then_inc(s["cchain"], 1)
            dve.wait_ge(s["cchain"], 1)
            v.tensor_scalar(ntile[:, :], ntok[:, :], float(P - 1), None, ALU.add).then_inc(s["cchain"], 1)
            dve.wait_ge(s["cchain"], 2)
            v.tensor_scalar(ntile[:, :], ntile[:, :], 7, None, ALU.logical_shift_right).then_inc(s["cchain"], 1)
            dve.wait_ge(s["cchain"], 3)
            v.tensor_scalar(ntile[:, :], ntile[:, :], float(MINT), None, ALU.max).then_inc(s["cchain"], 1)
            v.memset(tbase[:, 0:1], -1).then_inc(s["cchain"], 1)
            for e in range(E):
                dve.wait_ge(s["cchain"], 5 + e)
                v.tensor_tensor(tbase[:, e + 1:e + 2], tbase[:, e:e + 1], ntile[:, e:e + 1], ALU.add).then_inc(s["cchain"], 1)
            dve.wait_ge(s["cchain"], 5 + E)
            v.memset(zs[:, :, :], 0.0).then_inc(s["counts"], 1)

            def rows_lo(p):
                dve.wait_ge(s["rxh"], p + 3)
                lo(rT[:, 1, :], bQ[:, :], rT[:, 0, :]).then_inc(s["rxl"], 1)
                if not isinstance(p, int) or p > -1:
                    dve.wait_ge(s["mshift"], 2 * p + 2)
                elif p == -1:
                    dve.wait_ge(s["zrow"], 2)
                v.tensor_copy(meta[0][:, :], rowb[:, D:ROW].bitcast(U32)).then_inc(s["m0"], 1)

            def hidden_lo(p):
                dve.wait_ge(s["hh"], p + 1)
                lo(hT[:, 1, :], bT[:, :], hT[:, 0, :]).then_inc(s["hl"], 1)

            def hidden(t):
                dve.wait_ge(s["sgd"], t + 1)
                dve.wait_ge(s["up"], t + 1)
                dve.wait_ge(s["th2"], t) if not isinstance(t, int) or t > 0 else None
                v.tensor_tensor(hid, bS1[:, :], sg, ALU.mult).then_inc(s["hm"], 1)

            def accumulate(e, p):
                dve.wait_ge(s["dnp"], p + 1)
                dve.wait_ge(s["mshift"], 2 * p + 2)
                if not isinstance(p, int) or p > 0:
                    dve.wait_ge(s["sct"], 16 * p)
                v.tensor_scalar(acc, bO[:, :], meta[2][:, 1 + e:2 + e].bitcast(F32), None, ALU.mult).then_inc(s["accd"], 1)

            rows_lo(-2)
            for e in range(E):
                cnt = dve.value_load(ntile[0:1, e:e + 1], min_val=MINT, max_val=B * S // P)
                before = dve.value_load(tbase[0:1, e:e + 1], min_val=0, max_val=MAXT) if e else -1
                for k in range(2):
                    p = before + k
                    if e or k:
                        hidden_lo(p)
                    if e + 1 < E:
                        split_lo(e + 1, 3 * k)
                    hidden(p + 1)
                    rows_lo(p)
                    if e + 1 < E:
                        split_lo(e + 1, 3 * k + 1)
                    if e or k:
                        accumulate(e if k else e - 1, p)
                    if e + 1 < E:
                        split_lo(e + 1, 3 * k + 2)
                with dve.Fori(1, cnt - 1) as k:
                    p = before + 1 + k
                    hidden_lo(p)
                    hidden(p + 1)
                    rows_lo(p)
                    accumulate(e, p)
            last = dve.value_load(tbase[0:1, E:E + 1], min_val=0, max_val=MAXT)
            hidden_lo(last)
            accumulate(E - 1, last)

        @block.tensor
        def _(pe):
            te = nc.tensor

            def three(o, ws, xs, n):
                for c in range(n):
                    for at, (a, b) in enumerate(((0, 0), (0, 1), (1, 0))):
                        r = te.matmul(o, ws(a, c), xs(b, c), start=(c == 0 and at == 0),
                                      stop=(c == n - 1 and at == 2))
                return r

            def transposes(bank, src):
                for c in range(C):
                    r = te.transpose(bank[:, c * P:(c + 1) * P], src[:, c * P:(c + 1) * P], ident[:, :])
                return r

            cx = rflat[:, 4 * D:4 * D + C * B * KP].rearrange("p (c b n) -> p c b n", c=C, b=B)
            cr = rflat[:, 4 * D + C * B * KP:4 * D + C * B * KP + C * GK].rearrange("p (c n) -> p c n", c=C)
            wk_r = stage[:, 8 * D:12 * D].rearrange("p (c n) -> p c n", c=C)
            wv_r = rflat[:, 0:4 * D].rearrange("p (c n) -> p c n", c=C)
            pe.wait_ge(s["ld_wk"], 16)
            pe.wait_ge(s["ld_ctx"], 16 * B)
            for j in range(J):
                if j:
                    pe.wait_ge(s["kp_out"], j)
                for c in range(C):
                    r = te.matmul(bP[0][:, 0:B * KEYS].rearrange("p (b n) -> p b n", b=B),
                                  wk_r[:, c, j * P:(j + 1) * P], cx[:, c, :, 0:KEYS], start=(c == 0), stop=(c == C - 1))
                r.then_inc(s["kp"], 1)
            pe.wait_ge(s["ld_wv"], 16)
            pe.wait_ge(s["ld_small"], 16 * 5)
            pe.wait_ge(s["const_tiles"], 7)
            pe.wait_ge(s["kp_out"], J)
            for n in range(B * M):
                b, m = n // M, n % M
                pe.wait_ge(s["cr_done"], b + 1)
                if n >= 2:
                    pe.wait_ge(s["v_tmp"], n - 1)
                te.matmul(bP[n % 2][0:MK, :], ones1[0:1, 0:MK], vb_s[0:1, :], start=True, stop=False)
                for c in range(C):
                    r = te.matmul(bP[n % 2][0:MK, :], cr[:, c, m * MK:(m + 1) * MK], wv_r[:, c, :],
                                  start=False, stop=(c == C - 1))
                r.then_inc(s["vp"], 1)
            pe.wait_ge(s["v_tmp"], B * M)

            def scores(t, j):
                g, b = t // GT, (t % GT) // 2
                if t % GT == 0 and j == 0:
                    pe.wait_ge(s["ql"], 4 * (g + 1))
                if t == 0 and j == 0:
                    pe.wait_ge(s["k_lo"], J * HG)
                n = 4 * t + j
                if n >= 2:
                    pe.wait_ge(s["ma"], n - 1)
                cs = slice((t % GT) * P, (t % GT + 1) * P)
                q = qT[g % 2]
                three(bS[j % 2][:, 0:GK], lambda h, c: q[:, h, j, cs], lambda h, c: kbd[:, h, b, j, :], 1).then_inc(s["sp"], 1)

            def probs_T(t, j):
                n = 4 * t + j
                if j == 0:
                    pe.wait_ge(s["ex_done"], t + 1)
                if n >= 2:
                    pe.wait_ge(s["pl"], n - 1)
                for m in range(M):
                    at = j * GK + m * MK
                    r = te.transpose(bP[j % 2][0:MK, m * P:(m + 1) * P], smx[:, t % 2, at:at + MK], ident[:, :])
                r.then_inc(s["pt"], 1)

            def values(t, j):
                b = (t % GT) // 2
                pe.wait_ge(s["pl"], 4 * t + j + 1)
                if j % 2 == 0 and (t or j):
                    pe.wait_ge(s["cn"], 2 * t + j // 2)
                if t == 0 and j == 0:
                    pe.wait_ge(s["v_lo"], B * M)
                three(bV[:, (j % 2) * VC:(j % 2 + 1) * VC],
                      lambda h, m: pT[0:MK, j % 2, h, m * P:(m + 1) * P],
                      lambda h, m: vbd[0:MK, h, b, j, m, :], M).then_inc(s["pv"], 1)

            for st in STEPS:
                g, i = st // GT, st % GT
                if has(st):
                    scores(st, 0)
                    scores(st, 1)
                if has(st - 1):
                    probs_T(st - 1, 0)
                if has(st + 8):
                    t = st + 8
                    if t == 0:
                        pe.wait_ge(s["const_tiles"], 7)
                    pe.wait_ge(s["xn"], t + 1)
                    if t >= 1:
                        pe.wait_ge(s["xl"], t)
                    transposes(bT, xin[:, t % 4, :]).then_inc(s["tx"], 1)
                if has(st):
                    scores(st, 2)
                if has(st - 1):
                    probs_T(st - 1, 1)
                if has(st):
                    scores(st, 3)
                gq = g + 1
                if 0 <= gq < GROUPS:
                    if i == 0:
                        pe.wait_ge(s["xl"], 4 * gq + 4)
                    if gq == 0 and i == 0:
                        pe.wait_ge(s["wq_lo"], 1)
                    if gq or i:
                        pe.wait_ge(s["ql"], 4 * gq + i)
                    xx = xT[gq % 2]
                    three(bQ[:, :], lambda h, c: wq_s[:, h, c, i * P:(i + 1) * P], lambda h, c: xx[:, h, c, :], C).then_inc(s["qp"], 1)
                if has(st - 2):
                    t = st - 2
                    pe.wait_ge(s["cn"], 2 * t + 2)
                    pe.wait_ge(s["xl"], min(TILES, st + 9))
                    transposes(bT, ctok[:, t % 2, :]).then_inc(s["tc"], 1)
                if has(st - 1):
                    values(st - 1, 0)
                    values(st - 1, 1)
                    probs_T(st - 1, 2)
                    probs_T(st - 1, 3)
                if has(st - 3):
                    t = st - 3
                    pe.wait_ge(s["hn"], t + 1)
                    pe.wait_ge(s["cl"], min(TILES, st - 1))
                    transposes(bT, rows[:, (t // GT) % 2, t % GT, 0:D]).then_inc(s["th"], 1)
                if has(st - 2):
                    t = st - 2
                    pe.wait_ge(s["cl"], t + 1)
                    if t >= 1:
                        pe.wait_ge(s["x2d"], t)
                    if t >= 2:
                        pe.wait_ge(s["lgd"], t - 1)
                    if (st - 8) % GT == 0 and has(st - 8):
                        pe.wait_ge(s["rank_d"], (st - 8) // GT + 1)
                    if t == 0:
                        pe.wait_ge(s["wo_lo"], 1)
                    three(bO[:, :], lambda h, c: cT[:, h, c * P:(c + 1) * P], lambda h, c: wo_s[:, h, c, :], C).then_inc(s["op"], 1)
                if has(st - 1):
                    values(st - 1, 2)
                    values(st - 1, 3)
                if has(st - 3):
                    t = st - 3
                    pe.wait_ge(s["h2"], t + 1)
                    pe.wait_ge(s["x2d"], min(TILES, st - 1))
                    if t >= 1:
                        pe.wait_ge(s["lgd"], t)
                    for c in range(C):
                        r = te.matmul(LOGITS, h2T[:, c * P:(c + 1) * P], gw_s[:, c, :], start=(c == 0), stop=(c == C - 1))
                    r.then_inc(s["rt"], 1)
                gr = (st - 7) // GT
                if (st - 7) % GT == 0 and 0 <= gr < GROUPS:
                    pe.wait_ge(s["hot_d"], 3 * gr + 1)
                    pe.wait_ge(s["lgd"], st - 3)
                    te.matmul(RANK, tri[:, :], picked[:, :, :], start=True, stop=False)
                    for j in range(GT):
                        r = te.matmul(RANK[:, j + 1:GT + 1, :], ones[:, :],
                                      picked[:, j:j + 1, :].broadcast_to([P, GT - j, E]), start=False, stop=(j == GT - 1))
                    r.then_inc(s["rank"], 1)

            pe.wait_ge(s["counts"], 1)

            def rows_T(t):
                pe.wait_ge(s["rw"], 16 * t + 16)
                if not isinstance(t, int) or t > 0:
                    pe.wait_ge(s["rxl"], t)
                transposes(bQ, rowb[:, 0:D]).then_inc(s["tx2"], 1)

            def half(t, w, u):
                cs = slice(u * FF, (u + 1) * FF)
                return three(bS[u][:, :], lambda h, c: rT[:, h, c * P:(c + 1) * P], lambda h, c: w_gu[w][h][:, c, cs], C)

            def gates(t, w):
                pe.wait_ge(s["rxl"], t + 1)
                if not isinstance(t, int) or t > 0:
                    pe.wait_ge(s["sgd"], t)
                half(t, w, 0).then_inc(s["gt"], 1)

            def hidden_T(p):
                pe.wait_ge(s["hm"], p + 1)
                if not isinstance(p, int) or p > 0:
                    pe.wait_ge(s["hl"], p)
                transposes(bT, hid).then_inc(s["th2"], 1)

            def ups(t, w):
                half(t, w, 1).then_inc(s["up"], 1)

            def down(p, w):
                pe.wait_ge(s["hl"], p + 1)
                if not isinstance(p, int) or p > 0:
                    pe.wait_ge(s["accd"], p)
                three(bO[:, :], lambda h, c: hT[:, h, c * P:(c + 1) * P], lambda h, c: w_dn[w][h][:, c, :], C).then_inc(s["dnp"], 1)

            rows_T(0)
            for e in range(E):
                w = e % 2
                cnt = pe.value_load(ntile[0:1, e:e + 1], min_val=MINT, max_val=B * S // P)
                before = pe.value_load(tbase[0:1, e:e + 1], min_val=0, max_val=MAXT) if e else -1
                pe.wait_ge(s["wlo"], WCH * (e + 1))
                for k in range(2):
                    p = before + k
                    gates(p + 1, w)
                    if e or k:
                        hidden_T(p)
                    ups(p + 1, w)
                    rows_T(p + 2)
                    if e or k:
                        down(p, w if k else 1 - w)
                with pe.Fori(1, cnt - 1) as k:
                    p = before + 1 + k
                    gates(p + 1, w)
                    hidden_T(p)
                    ups(p + 1, w)
                    rows_T(p + 2)
                    down(p, w)
            last = pe.value_load(tbase[0:1, E:E + 1], min_val=0, max_val=MAXT)
            hidden_T(last)
            down(last, (E - 1) % 2)


_INS = ["x", "ctxT", "mask", "wq", "q_b", "wk", "k_b", "wv", "v_b", "wo", "o_b", "gw", "gu", "dn"]


def kernel(x, ctx_1024, mask_SxS2_bk1, L0_xattn_q_w, L0_xattn_q_b, L0_xattn_k_w, L0_xattn_k_b,
           L0_xattn_v_w, L0_xattn_v_b, L0_xattn_o_w, L0_xattn_o_b, L0_ffn_gate_w, L0_ffn_gate_up_proj,
           L0_ffn_down_proj):
    import numpy as np
    import concourse.bacc as bacc
    from concourse.bass_utils import run_bass_kernel_spmd

    def rows_first(a):
        a = np.asarray(a)
        return np.ascontiguousarray(a.reshape(-1, P, a.shape[1]).transpose(1, 0, 2))

    def by_head_group(b):
        return np.ascontiguousarray(np.asarray(b).reshape(J, P).T)

    def turned(w):
        return rows_first(np.asarray(w).T)

    given = {
        "x": x, "ctxT": np.stack([turned(c) for c in np.asarray(ctx_1024)]),
        "mask": rows_first(mask_SxS2_bk1),
        "wq": turned(L0_xattn_q_w), "q_b": by_head_group(L0_xattn_q_b),
        "wk": turned(L0_xattn_k_w), "k_b": by_head_group(L0_xattn_k_b),
        "wv": turned(L0_xattn_v_w), "v_b": L0_xattn_v_b, "wo": turned(L0_xattn_o_w), "o_b": L0_xattn_o_b,
        "gw": turned(L0_ffn_gate_w), "gu": L0_ffn_gate_up_proj, "dn": L0_ffn_down_proj,
    }
    nc = bacc.Bacc("TRN2", target_bir_lowering=False, num_devices=1)
    arrays, args = {}, []
    for name in _INS:
        a = np.ascontiguousarray(given[name])
        arrays[f"in_{name}"] = a
        args.append(nc.dram_tensor(f"in_{name}", a.shape, mybir.dt.from_np(a.dtype), kind="ExternalInput").ap())
    args.append(nc.dram_tensor("out_0", (B, S, D), F32, kind="ExternalOutput").ap())
    build(nc, *args)
    r = run_bass_kernel_spmd(nc, [arrays], core_ids=[0])
    return r.results[0]["out_0"]
```

```python
from contextlib import ExitStack

import concourse.bass as bass
from concourse import mybir

P = 128
F32 = mybir.dt.float32
F32R = mybir.dt.float32r
BF16 = mybir.dt.bfloat16
I32 = mybir.dt.int32
U32 = mybir.dt.uint32
U8 = mybir.dt.uint8
ALU = mybir.AluOpType
ACT = mybir.ActivationFunctionType
AX = mybir.AxisListType

B, S, D = 2, 2048, 512
KEYS, HEADS, HD = 77, 16, 32
KP = KEYS + 1
E, FF = 8, 512
LN_EPS, TOPK_EPS = 1e-5, 1e-9
C = D // P
HG = P // HD
J = HEADS // HG
GK = HG * KP
M = 3
MK = GK // M
VC = P + HG
VW = VC + P
TILES = B * S // P
GT = 4
GROUPS = TILES // GT
ROW = D + 1 + E
MINT = 3
REG = B * S + MINT * P
NOBODY = 8191
WCH = 6
MAXT = 2 * TILES + MINT * E
SCALE = 1.0 / float(HD) ** 0.5
MASKED = -1e30
assert GK % M == 0 and GK % 2 == 0


def build(nc, x, ctxT, mask, wq, q_b, wk, k_b, wv, v_b, wo, o_b, gw, gu, dn, out):
    with ExitStack() as ctx:
        def sb(name, shape, dt=F32):
            return ctx.enter_context(nc.sbuf_tensor(name, shape, dt))

        def sem(name):
            return ctx.enter_context(nc.semaphore(name))

        slots = nc.dram_tensor("slots", [E * REG, ROW], F32, kind="Internal").ap()
        xr_rows = x.rearrange("b s d -> (b s) d")
        out_rows = out.rearrange("b s d -> (b s) d")

        WE = C * (2 * FF) + C * D
        ops = sb("ops", [P, 4 * WE], F32R)
        CD = C * GT * P

        def part(at, inner):
            v = ops[:, at:at + 2 * CD].rearrange("p (h c n) -> p h c n", h=2, c=C)
            assert v.shape[3] == inner
            return v

        xT = [part(q * 2 * CD, 512) for q in range(2)]
        wq_s = part(4 * CD, D)
        qT = [part(6 * CD + q * 2 * CD, 512) for q in range(2)]
        wo_s = part(10 * CD, D)
        w_gu = [[ops[:, (2 * w + h) * WE:(2 * w + h) * WE + C * 2 * FF].rearrange("p (c n) -> p c n", c=C)
                 for h in range(2)] for w in range(2)]
        w_dn = [[ops[:, (2 * w + h) * WE + C * 2 * FF:(2 * w + h + 1) * WE].rearrange("p (c n) -> p c n", c=C)
                 for h in range(2)] for w in range(2)]
        kbd = sb("kbd", [P, 2 * B * J * GK], F32R)[:, :].rearrange("p (h b j n) -> p h b j n", h=2, b=B, j=J)
        kflat = kbd.rearrange("p h b j n -> p (h b j n)")
        vbd = sb("vbd", [P, B * J * M * VW], F32R)[:, :].rearrange("p (b j m n) -> p b j m n", b=B, j=J, m=M)
        pT = sb("pT", [P, 2, 2, M * P], F32R)
        cT = sb("cT", [P, 2, C * P], F32R)
        rT = kflat[:, 0:2 * D].rearrange("p (h n) -> p h n", h=2)
        hT = cT

        stage = sb("stage", [P, WCH * 1024])
        xin = stage[:, 0:4 * D].rearrange("p (t n) -> p t n", t=4)
        SMW = HEADS * KP
        smx = stage[:, 4 * D:4 * D + 2 * SMW].rearrange("p (t n) -> p t n", t=2)
        c_at = 4 * D + 2 * SMW
        ctok = stage[:, c_at:c_at + 2 * D].rearrange("p (t n) -> p t n", t=2)
        h2T = stage[:, c_at + 2 * D:c_at + 3 * D]
        wraw = stage[:, :].rearrange("p (w n) -> p w n", w=WCH)
        xres = sb("xres", [P, 2, D])
        x2 = sb("x2", [P, 2, D])
        rows = sb("rows", [P, 2, GT, ROW])
        rflat = rows[:, :, :, :].rearrange("p q t n -> p (q t n)")
        mbias = sb("mbias", [P, S // P, KP], BF16)
        mraw = xres[:, 0, :].bitcast(U8)[:, 0:S // P * KP].rearrange("p (t n) -> p t n", n=KP)
        ident = sb("ident", [P, P])
        tri = sb("tri", [P, P], BF16)
        ones = sb("ones", [P, P], BF16)
        gw_s = sb("gw_s", [P, C, E])
        qb_s = sb("qb_s", [P, J])
        kb_s = sb("kb_s", [P, J])
        vb_s = x2[0:1, 1, :]
        ktmps = [x2[:, 0, n * B * KEYS:(n + 1) * B * KEYS].rearrange("p (b n) -> p b n", b=B) for n in range(2)]
        ones1 = x2[0:1, 0, 3 * P:4 * P]
        ob_s = sb("ob_s", [P, D])
        hsel = sb("hsel", [P, M, HG])
        toki = sb("toki", [P, TILES], U32)
        iota8i = sb("iota8i", [P, E], I32)
        iota8 = sb("iota8", [P, E])
        firsti = sb("firsti", [P, E], I32)
        first = sb("first", [P, E])
        mhalf = sb("mhalf", [P, 1])
        st1, mv1, ve1, rs1, nm1 = (sb(n, [P, 4, w]) for n, w in
                                   (("st1", 6), ("mv1", 2), ("ve1", 1), ("rs1", 1), ("nm1", 1)))
        st2, mv2, ve2, rs2, nm2 = (sb(n, [P, 4, w]) for n, w in
                                   (("st2", 6), ("mv2", 2), ("ve2", 1), ("rs2", 1), ("nm2", 1)))
        mxs = sb("mxs", [P, 2, HEADS])
        rden = sb("rden", [P, J, HG])
        lg = sb("lg", [P, 2, GT, E])
        top = sb("top", [P, GT, E])
        topi = sb("topi", [P, GT, E], U32)
        topf = sb("topf", [P, GT, 2])
        hot = sb("hot", [P, 2, GT, E])
        picked = sb("picked", [P, GT + 1, E], BF16)
        dif = sb("dif", [P, GT, E])
        ex = sb("ex", [P, GT, E])
        zs = sb("zs", [P, GT, 1])
        rz = sb("rz", [P, GT, 1])
        pp = sb("pp", [P, GT, 2])
        rank = sb("rank", [P, GT + 1, E])
        count = sb("count", [P, E])
        slot = sb("slot", [P, GT, E])
        tmp = sb("tmp", [P, 2, GT, E])
        slotf = sb("slotf", [P, 2, GT])
        sloti = sb("sloti", [P, 2, 2, GT], U32)
        ntok = sb("ntok", [P, E], I32)
        ntile = sb("ntile", [P, E], I32)
        tbase = sb("tbase", [P, E + 1], I32)
        emptyrow = rflat[:, (2 * GT - 1) * ROW:2 * GT * ROW]
        padrow = rflat[:, ROW:2 * ROW]
        rowb = rflat[:, 0:ROW]
        sg = xres[:, 0, :]
        hid = xres[:, 1, :]
        acc = x2[:, 1, :]
        meta = [sb(f"meta{n}", [P, 1 + E], U32) for n in range(3)]
        zero = sb("zero", [P, 1 + E], U32)
        idle = sb("idle", [P, 1], U32)

        bT, bQ, bS0, bS1, bP0, bP1, bV, bO = (
            ctx.enter_context(nc.psum_tensor(n, [P, 512], F32))
            for n in ("bT", "bQ", "bS0", "bS1", "bP0", "bP1", "bV", "bO"))
        bS, bP = [bS0, bS1], [bP0, bP1]
        LOGITS = bO[:, 0:E]
        RANK = bO[:, E:E + (GT + 1) * E].rearrange("p (t e) -> p t e", e=E)

        names = """
        ld_wq ld_wo ld_wk ld_wv ld_ctx ld_mask ld_small ld_kb mraw_set ctx_pad consts const_tiles
        cr_done wq_hi wq_lo wo_hi wo_lo kp kp_out kz k_hi k_lo vp v_tmp v_hi v_lo tok_done
        ln1 rs1d nm1d xn tx xh xl qp qh ql sp ma mxd sub ex_done pt ph pl pv rc c_lo csum cn tc ch cl op
        xb x2d ln2 rs2d nm2d hn th h2 rt lgd route dif_d exr hot_d rank prow pre_pads rank_d
        counts pads zrow cchain
        rw whi wlo gt sgd th2 hh hl up hm tx2 rxh rxl dnp accd sct mshift m0""".split()
        s = {n: sem(n) for n in names}
        x_in = [sem(f"x_in{i}") for i in range(4)]
        xr_in = [sem(f"xr_in{i}") for i in range(2)]
        x_st = [sem(f"x_st{i}") for i in range(2)]
        scat = [sem(f"scat{i}") for i in range(GT)]
        w_in = [sem(f"w_in{i}") for i in range(WCH)]

        def rows_of(g, i):
            return (i // 2) * S + (2 * g + i % 2) * P

        block = ctx.enter_context(nc.Block())

        STEPS = range(-9, TILES + 11)

        def has(t):
            return 0 <= t < TILES

        V_STEP = -B * M - 2
        WQ_STEP = STEPS[0]

        W0_STEP = TILES - GT

        def w_slot(e, ch):
            return ch if e else ch % 2

        def w_loads(e, ch):
            if e == 0:
                return ch // 2 + 1
            return e + (WCH // 2 if ch < 2 else 0)

        def n_before(e, ch):
            if e == 0:
                return max(0, ch - 1)
            if e == 1:
                return ch + WCH - 1 if ch < 2 else 0
            return WCH * (e - 1) + ch + 1

        def load_w(eng, e, ch):
            at = w_slot(e, ch)
            if n_before(e, ch):
                eng.wait_ge(s["wlo"], n_before(e, ch))
            if ch < 4:
                eng.dma_start(wraw[:, at, :], gu[e, ch * P:(ch + 1) * P, :]).then_inc(w_in[at], 16)
            else:
                eng.dma_start(wraw[:, at, :].rearrange("p (c n) -> p c n", c=2),
                              dn[e].rearrange("(c p) n -> p c n", p=P)[:, 2 * (ch - 4):2 * (ch - 4) + 2, :]).then_inc(w_in[at], 16)

        ROUTE_STEPS = 2 * GT + 20

        @block.sync
        def _(sp):
            sp.dma_start(stage[:, 8 * D:12 * D].rearrange("p (c n) -> p c n", c=C),
                         wk).then_inc(s["ld_wk"], 16)
            cx = rflat[:, 4 * D:4 * D + C * B * KP].rearrange("p (c b n) -> p c b n", c=C, b=B)
            sp.wait_ge(s["ctx_pad"], 1)
            for b in range(B):
                sp.dma_start(cx[:, :, b, 0:KEYS], ctxT[b]).then_inc(s["ld_ctx"], 16)

            def load_x(t):
                g, i = t // GT, t % GT
                if t >= 4:
                    sp.wait_ge(s["tx"], t - 3)
                sp.dma_start(xin[:, i, :], xr_rows[bass.ds(rows_of(g, i), P), :]).then_inc(x_in[i], 16)

            for t in range(4):
                load_x(t)
            sp.dma_start(stage[:, 4 * D:8 * D].rearrange("p (c n) -> p c n", c=C),
                         wq).then_inc(s["ld_wq"], 16)
            sp.dma_start(rflat[:, 0:4 * D].rearrange("p (c n) -> p c n", c=C),
                         wv).then_inc(s["ld_wv"], 16)
            for st in STEPS:
                if 4 <= st + 12 < TILES:
                    load_x(st + 12)
                if st == WQ_STEP + 1:
                    sp.wait_ge(s["wq_lo"], 1)
                    sp.dma_start(stage[:, 4 * D:8 * D].rearrange("p (c n) -> p c n", c=C),
                                 wo).then_inc(s["ld_wo"], 16)
                if has(st):
                    i = st % GT
                    if st >= 2:
                        sp.wait_ge(s["x2d"], st - 1)
                    elif st == 0:
                        sp.wait_ge(s["v_lo"], 2 * M)
                    sp.dma_start(xres[:, st % 2, :], xr_rows[bass.ds(rows_of(st // GT, i), P), :]).then_inc(xr_in[st % 2], 16)
                if has(st - 2):
                    t = st - 2
                    sp.wait_ge(s["x2d"], t + 1)
                    sp.dma_start(out_rows[bass.ds(rows_of(t // GT, t % GT), P), :], x2[:, t % 2, :]).then_inc(x_st[t % 2], 16)
                if 0 <= st < E:
                    if st == 0:
                        sp.wait_ge(s["prow"], 2)
                    sp.dma_start(slots[st * REG:st * REG + MINT * P, :].rearrange("(k p) n -> p k n", p=P),
                                 emptyrow[:, None, :].broadcast_to([P, MINT, ROW])).then_inc(s["pre_pads"], 16)
                if st == W0_STEP - 1:
                    sp.wait_ge(s["tx"], TILES)
                    load_w(sp, 0, 0)
                    load_w(sp, 0, 1)
                if W0_STEP < st < W0_STEP + WCH - 1:
                    load_w(sp, 0, st - W0_STEP + 1)

            def pad(e):
                n = sp.value_load(ntok[0:1, e:e + 1], min_val=0, max_val=B * S)
                sp.dma_start(slots[bass.ds(n + e * REG, P), :], padrow).then_inc(s["pads"], 16)

            sp.wait_ge(s["counts"], 1)
            sp.wait_ge(s["prow"], 4)
            pad(0)
            sp.wait_ge(s["pads"], 16)
            for q in scat:
                sp.wait_ge(q, 16 * 2 * GROUPS)

            def load_rows(e, k, t):
                if not isinstance(t, int) or t > 0:
                    sp.wait_ge(s["tx2"], t)
                    sp.wait_ge(s["m0"], t)
                sp.dma_start(rowb, slots[bass.ds(k * P + e * REG, P), :]).then_inc(s["rw"], 16)

            for e in range(E):
                cnt = sp.value_load(ntile[0:1, e:e + 1], min_val=MINT, max_val=B * S // P)
                base = 1 + sp.value_load(tbase[0:1, e:e + 1], min_val=0, max_val=MAXT) if e else 0
                if e == 1:
                    sp.wait_ge(s["pads"], 16 * E)
                load_rows(e, 0, base)
                if e == 0:
                    sp.wait_ge(s["pt"], TILES * J)
                    sp.wait_ge(s["tc"], TILES)
                    sp.wait_ge(s["rt"], TILES)
                    for ch in range(WCH // 2):
                        load_w(sp, 1, ch)
                load_rows(e, 1, base + 1)
                if e == 0:
                    for ch in range(WCH // 2, WCH):
                        load_w(sp, 1, ch)
                    for n in range(1, E):
                        pad(n)
                with sp.Fori(2, cnt) as k:
                    load_rows(e, k, base + k)
            tend = 1 + sp.value_load(tbase[0:1, E:E + 1], min_val=0, max_val=MAXT)
            load_rows(0, 0, tend)

        @block.gpsimd
        def _(pool):
            g_ = nc.gpsimd
            g_.memset(kflat.bitcast(F32), 0.0).then_inc(s["kz"], 1)
            pool.dma_start(gw_s[:, :, :], gw).then_inc(s["ld_small"], 16)
            pool.dma_start(qb_s[:, :], q_b).then_inc(s["ld_small"], 16)
            pool.dma_start(vb_s[:, :], v_b[None, :]).then_inc(s["ld_small"], 16)
            pool.dma_start(ob_s[:, :], o_b[None, :].broadcast_to([P, D])).then_inc(s["ld_small"], 16)
            g_.memset(ident[:, :], 0.0).then_inc(s["consts"], 1)
            g_.memset(tri[:, :], 1.0).then_inc(s["consts"], 1)
            g_.memset(hsel[:, :, :], 1.0).then_inc(s["consts"], 1)
            g_.memset(ones[:, :], 1.0).then_inc(s["const_tiles"], 1)
            g_.memset(ones1[:, :], 1.0).then_inc(s["const_tiles"], 1)
            g_.memset(mhalf[:, :], -0.5).then_inc(s["const_tiles"], 1)
            pool.wait_ge(s["consts"], 3)
            g_.affine_select(out=ident[:, :], in_=ident[:, :], compare_op=ALU.not_equal, fill=1.0, base=0,
                             pattern=[[-1, P]], channel_multiplier=1).then_inc(s["const_tiles"], 1)
            g_.affine_select(out=tri[:, :], in_=tri[:, :], compare_op=ALU.is_gt, fill=0.0, base=0,
                             pattern=[[1, P]], channel_multiplier=-1).then_inc(s["const_tiles"], 1)
            g_.affine_select(out=hsel[:, :, :], in_=hsel[:, :, :], compare_op=ALU.is_ge, fill=0.0, base=0,
                             pattern=[[MK, M], [-KP, HG]], channel_multiplier=1).then_inc(s["consts"], 1)
            pool.wait_ge(s["consts"], 4)
            g_.affine_select(out=hsel[:, :, :], in_=hsel[:, :, :], compare_op=ALU.is_ge, fill=0.0, base=KP - 1,
                             pattern=[[-MK, M], [KP, HG]], channel_multiplier=-1).then_inc(s["const_tiles"], 1)
            g_.iota(toki[:, :], pattern=[[2 * P, GROUPS], [S, 2], [P, 2]], base=0, channel_multiplier=1).then_inc(s["tok_done"], 1)
            g_.iota(iota8i[:, :], pattern=[[1, E]], base=0, channel_multiplier=0).then_inc(s["tok_done"], 1)
            g_.iota(firsti[:, :], pattern=[[REG, E]], base=0, channel_multiplier=0).then_inc(s["tok_done"], 1)
            g_.memset(picked[:, GT, :], 0.0).then_inc(s["const_tiles"], 1)

            def rstd(t, ve, rs, mv, nm, from_, rsd, nmd, per):
                i = t % 4
                pool.wait_ge(s[from_], per * t + per)
                g_.tensor_tensor(rs[:, i, :], ve[:, i, :], mhalf[:, :], ALU.pow).then_inc(s[rsd], 1)
                pool.wait_ge(s[rsd], t + 1)
                g_.tensor_scalar(nm[:, i, :], mv[:, i, 0:1], rs[:, i, 0:1], -1.0, ALU.mult, ALU.mult).then_inc(s[nmd], 1)

            for st in STEPS:
                if st == TILES + 6:
                    pool.wait_ge(scat[1], 16 * 2 * (GROUPS - 1))
                    g_.memset(padrow, 0.0).then_inc(s["prow"], 1)
                    pool.wait_ge(s["prow"], 3)
                    g_.memset(padrow[:, D:D + 1].bitcast(U32), NOBODY).then_inc(s["prow"], 1)
                if has(st - 11):
                    gs, i = (st - 11) // GT, (st - 11) % GT
                    if i == 0:
                        pool.wait_ge(s["route"], ROUTE_STEPS * (gs + 1))
                    if st == 11:
                        pool.wait_ge(s["pre_pads"], 16 * E)
                    if gs:
                        pool.wait_ge(scat[i], 16 * 2 * gs)
                    for k in range(2):
                        pool.indirect_dma_start(
                            out=slots[:, :], out_offset=bass.IndirectOffsetOnAxis(ap=sloti[:, gs % 2, k, i:i + 1], axis=0),
                            in_=rows[:, gs % 2, i, :], in_offset=None).then_inc(scat[i], 16)
                if has(st - 3):
                    rstd(st - 3, ve2, rs2, mv2, nm2, "ln2", "rs2d", "nm2d", 3)
                if has(st - 1):
                    t = st - 1
                    if t == 0:
                        pool.wait_ge(s["ld_small"], 16 * 4)
                    pool.wait_ge(xr_in[t % 2], 16 * (t // 2 + 1))
                    g_.tensor_tensor(xres[:, t % 2, :], xres[:, t % 2, :], ob_s[:, :], ALU.add).then_inc(s["xb"], 1)
                if st == 0:
                    pool.wait_ge(s["vp"], B * M)
                    g_.memset(emptyrow, 0.0).then_inc(s["prow"], 1)
                    pool.wait_ge(s["prow"], 1)
                    g_.memset(emptyrow[:, D:D + 1].bitcast(U32), NOBODY).then_inc(s["prow"], 1)
                if has(st):
                    pool.wait_ge(s["mxd"], st + 1)
                    v = smx[:, st % 2, :].rearrange("p (h n) -> p h n", h=HEADS)
                    g_.tensor_tensor(v, v, mxs[:, st % 2, :, None].broadcast_to([P, HEADS, KP]),
                                     ALU.subtract).then_inc(s["sub"], 1)
                if has(st + 9):
                    if st + 9 == 0:
                        pool.wait_ge(s["const_tiles"], 3)
                    rstd(st + 9, ve1, rs1, mv1, nm1, "ln1", "rs1d", "nm1d", 3)

            for q in x_st:
                pool.wait_ge(q, 16 * TILES // 2)

            def idle_add():
                g_.tensor_tensor(idle[:, :], zero[:, 0:1], zero[:, 0:1], ALU.add)

            def combine(t):
                pool.wait_ge(s["accd"], t + 1)
                idle_add()
                pool.indirect_dma_start(
                    out=out_rows[:, :], out_offset=bass.IndirectOffsetOnAxis(ap=meta[2][:, 0:1], axis=0),
                    in_=acc, in_offset=None, compute_op=ALU.add,
                    bounds_check=B * S - 1, oob_is_err=False).then_inc(s["sct"], 16)
                pool.wait_ge(s["sct"], 16 * t + 16)

            def move(to, of):
                return g_.tensor_tensor(meta[to][:, :], meta[of][:, :], zero[:, :], ALU.add)

            def shift(t):
                pool.wait_ge(s["m0"], t + 2)
                move(2, 1).then_inc(s["mshift"], 1)
                pool.wait_ge(s["mshift"], 2 * t + 1)
                move(1, 0).then_inc(s["mshift"], 1)

            pool.wait_ge(s["m0"], 1)
            g_.memset(zero[:, :], 0).then_inc(s["zrow"], 1)
            pool.wait_ge(s["zrow"], 1)
            move(1, 0).then_inc(s["zrow"], 1)
            pool.wait_ge(s["counts"], 1)
            for e in range(E):
                cnt = pool.value_load(ntile[0:1, e:e + 1], min_val=MINT, max_val=B * S // P)
                base = 1 + pool.value_load(tbase[0:1, e:e + 1], min_val=0, max_val=MAXT) if e else 0
                with pool.Fori(0, cnt) as k:
                    shift(base + k)
                    combine(base + k)
            tend = 1 + pool.value_load(tbase[0:1, E:E + 1], min_val=0, max_val=MAXT)
            pool.wait_ge(s["sct"], 16 * tend)

        @block.scalar
        def _(act):
            a = nc.scalar

            def copy(o, i):
                return a.activation(o, i, ACT.Copy)

            def ph(t, j):
                n = 4 * t + j
                act.wait_ge(s["pt"], n + 1)
                if n >= 2:
                    act.wait_ge(s["pv"], n - 1)
                copy(pT[0:MK, j % 2, 0, :], bP[j % 2][0:MK, 0:M * P]).then_inc(s["ph"], 1)

            act.dma_start(kb_s[:, :], k_b).then_inc(s["ld_kb"], 16)
            act.wait_ge(s["mraw_set"], 1)
            act.dma_start(mraw[:, :, 0:KEYS], mask).then_inc(s["ld_mask"], 16)
            act.wait_ge(s["ld_kb"], 16)
            for j in range(J):
                ktmp = ktmps[j % 2]
                act.wait_ge(s["kp"], j + 1)
                if j >= 2:
                    act.wait_ge(s["k_lo"], HG * (j - 1))
                a.activation(ktmp, bP[j % 2][:, 0:B * KEYS].rearrange("p (b n) -> p b n", b=B), ACT.Identity,
                             bias=kb_s[:, j:j + 1]).then_inc(s["kp_out"], 1)
                act.wait_ge(s["kp_out"], j + 1)
                if j == 0:
                    act.wait_ge(s["kz"], 1)
                for h in range(HG):
                    rs = slice(h * HD, (h + 1) * HD)
                    copy(kbd[rs, 0, :, j, h * KP:h * KP + KEYS], ktmp[rs]).then_inc(s["k_hi"], 1)
            def context_lo(t, j):
                act.wait_ge(s["pv"], 4 * t + j + 1)
                if t >= 2 and j == 0:
                    act.wait_ge(s["tc"], t - 1)
                copy(ctok[:, t % 2, j * P:(j + 1) * P], (bV if j % 2 == 0 else bQ)[:, VC:VW]).then_inc(s["c_lo"], 1)

            def value_hi(n):
                b, m = n // M, n % M
                act.wait_ge(s["v_tmp"], n + 1)
                vt = xres[0:MK, n % 2, :].rearrange("p (j n) -> p j n", j=J)
                copy(vbd[0:MK, b, :, m, 0:P], vt).then_inc(s["v_hi"], 1)

            def split_hi(e, ch):
                act.wait_ge(w_in[w_slot(e, ch)], 16 * w_loads(e, ch))
                w = e % 2
                dst = (w_gu[w][0][:, ch, :] if ch < 4 else
                       w_dn[w][0][:, 2 * (ch - 4):2 * (ch - 4) + 2, :].rearrange("p c n -> p (c n)"))
                copy(dst, wraw[:, w_slot(e, ch), :]).then_inc(s["whi"], 1)

            def norm(t, dst, src, rs, nm):
                i = t % 4
                return a.activation(dst, src, ACT.Identity, scale=rs[:, i, 0:1], bias=nm[:, i, 0:1])

            def norm_x(t):
                act.wait_ge(s["nm1d"], t + 1)
                norm(t, xin[:, t % 4, :], xin[:, t % 4, :], rs1, nm1).then_inc(s["xn"], 1)

            for st in STEPS:
                g, i = st // GT, st % GT
                if has(st - 1):
                    ph(st - 1, 0)
                if has(st + 8):
                    t = st + 8
                    act.wait_ge(s["tx"], t + 1)
                    if t >= 8 and t % GT == 0:
                        act.wait_ge(s["qp"], 4 * (t // GT - 1))
                    copy(xT[(t // GT) % 2][:, 0, :, (t % GT) * P:(t % GT + 1) * P],
                         bT[:, :].rearrange("p (c n) -> p c n", c=C)).then_inc(s["xh"], 1)
                if has(st - 1):
                    ph(st - 1, 1)
                if st < 0:
                    norm_x(st + 9)
                gq = g + 1
                if st == WQ_STEP:
                    act.wait_ge(s["ld_wq"], 16)
                    copy(wq_s[:, 0].rearrange("p c n -> p (c n)"), stage[:, 4 * D:8 * D]).then_inc(s["wq_hi"], 1)
                if st == -GT:
                    act.wait_ge(s["ld_small"], 16 * 4)
                if st == -1:
                    act.wait_ge(s["ld_wo"], 16)
                    copy(wo_s[:, 0].rearrange("p c n -> p (c n)"), stage[:, 4 * D:8 * D]).then_inc(s["wo_hi"], 1)
                if 0 <= gq < GROUPS:
                    act.wait_ge(s["qp"], 4 * gq + i + 1)
                    if gq >= 2 and i == 0:
                        act.wait_ge(s["sp"], 16 * (gq - 1))
                    a.activation(qT[gq % 2][:, 0, i, :], bQ[:, :], ACT.Identity,
                                 bias=qb_s[:, i:i + 1]).then_inc(s["qh"], 1)
                if has(st - 2):
                    t = st - 2
                    act.wait_ge(s["tc"], t + 1)
                    if t >= 1:
                        act.wait_ge(s["op"], t)
                    copy(cT[:, 0, :], bT[:, :]).then_inc(s["ch"], 1)
                if 0 <= st - V_STEP < B * M:
                    value_hi(st - V_STEP)
                if has(st - 3):
                    t = st - 3
                    act.wait_ge(s["nm2d"], t + 1)
                    act.wait_ge(s["x2d"], t + 1)
                    if t == 2 * GT - 1:
                        act.wait_ge(s["pre_pads"], 16 * E)
                    if t >= 2 * GT:
                        act.wait_ge(scat[t % GT], 16 * 2 * (t // GT - 1))
                    norm(t, rows[:, (t // GT) % 2, t % GT, 0:D], x2[:, t % 2, :], rs2, nm2).then_inc(s["hn"], 1)
                if has(st - 1):
                    context_lo(st - 1, 0)
                    ph(st - 1, 2)
                    context_lo(st - 1, 1)
                    ph(st - 1, 3)
                if has(st):
                    act.wait_ge(s["sub"], st + 1)
                    a.activation(smx[:, st % 2, :], smx[:, st % 2, :], ACT.Exp, scale=SCALE).then_inc(s["ex_done"], 1)
                if has(st - 3):
                    act.wait_ge(s["th"], st - 2)
                    if st - 3 >= 1:
                        act.wait_ge(s["rt"], st - 3)
                    copy(h2T, bT[:, :]).then_inc(s["h2"], 1)
                if has(st - 1):
                    context_lo(st - 1, 2)
                    context_lo(st - 1, 3)
                if st >= 0 and has(st + 9):
                    norm_x(st + 9)
                if 0 <= st - W0_STEP < WCH:
                    if st == W0_STEP:
                        act.wait_ge(s["qp"], 4 * GROUPS)
                    split_hi(0, st - W0_STEP)
                gr = (st - 7) // GT
                if (st - 7) % GT == 0 and 0 <= gr < GROUPS:
                    act.wait_ge(s["dif_d"], gr + 1)
                    a.activation(ex[:, :, :], dif[:, :, :], ACT.Exp).then_inc(s["exr"], 1)

            act.wait_ge(s["op"], TILES)
            act.wait_ge(s["counts"], 1)

            def silu(t):
                act.wait_ge(s["gt"], t + 1)
                if not isinstance(t, int) or t > 0:
                    act.wait_ge(s["hm"], t)
                a.activation(sg, bS0[:, :], ACT.Silu).then_inc(s["sgd"], 1)

            def hidden_hi(p):
                act.wait_ge(s["th2"], p + 1)
                if not isinstance(p, int) or p > 0:
                    act.wait_ge(s["dnp"], p)
                copy(hT[:, 0, :], bT[:, :]).then_inc(s["hh"], 1)

            def rows_hi(t):
                act.wait_ge(s["tx2"], t + 1)
                if not isinstance(t, int) or t > 0:
                    act.wait_ge(s["up"], t)
                copy(rT[:, 0, :], bQ[:, :]).then_inc(s["rxh"], 1)

            rows_hi(0)
            for e in range(E):
                cnt = act.value_load(ntile[0:1, e:e + 1], min_val=MINT, max_val=B * S // P)
                before = act.value_load(tbase[0:1, e:e + 1], min_val=0, max_val=MAXT) if e else -1
                for k in range(2):
                    p = before + k
                    silu(p + 1)
                    if e or k:
                        hidden_hi(p)
                    if e + 1 < E:
                        if k == 0 and e:
                            act.wait_ge(s["up"], p + 1)
                        split_hi(e + 1, 3 * k)
                    rows_hi(p + 2)
                    if e + 1 < E:
                        if k == 1 and e:
                            act.wait_ge(s["dnp"], p)
                        split_hi(e + 1, 3 * k + 1)
                        split_hi(e + 1, 3 * k + 2)
                if e + 2 < E:
                    for ch in range(WCH):
                        load_w(act, e + 2, ch)
                with act.Fori(1, cnt - 1) as k:
                    p = before + 1 + k
                    silu(p + 1)
                    hidden_hi(p)
                    rows_hi(p + 2)
            last = act.value_load(tbase[0:1, E:E + 1], min_val=0, max_val=MAXT)
            hidden_hi(last)

        @block.vector
        def _(dve):
            v = nc.vector

            def f(ap):
                return ap.bitcast(F32)

            def lo(dst, full, hi):
                return v.tensor_tensor(dst, full, f(hi), ALU.subtract)

            cx = rflat[:, 4 * D:4 * D + C * B * KP].rearrange("p (c b n) -> p c b n", c=C, b=B)
            cr = rflat[:, 4 * D + C * B * KP:4 * D + C * B * KP + C * GK].rearrange("p (c h n) -> p c h n", c=C, h=HG)
            v.memset(rflat[:, 4 * D:4 * D + C * B * KP], 0.0).then_inc(s["ctx_pad"], 1)
            v.memset(mraw[:, :, :], 1).then_inc(s["mraw_set"], 1)
            dve.wait_ge(s["tok_done"], 3)
            v.tensor_copy(iota8[:, :], iota8i[:, :]).then_inc(s["tok_done"], 1)
            v.tensor_copy(count[:, :], firsti[:, :]).then_inc(s["tok_done"], 1)
            v.tensor_copy(first[:, :], firsti[:, :]).then_inc(s["tok_done"], 1)

            def ln(t, src, stt, mv, ve, name):
                i = t % 4
                v.bn_stats(stt[:, i, :], src).then_inc(s[name], 1)
                dve.wait_ge(s[name], 3 * t + 1)
                v.bn_aggr(mv[:, i, :], stt[:, i, :]).then_inc(s[name], 1)
                dve.wait_ge(s[name], 3 * t + 2)
                v.tensor_scalar(ve[:, i, :], mv[:, i, 1:2], LN_EPS, None, ALU.add).then_inc(s[name], 1)

            def ln_x(t):
                dve.wait_ge(x_in[t % 4], 16 * (t // 4 + 1))
                ln(t, xin[:, t % 4, :], st1, mv1, ve1, "ln1")

            def repeat_rows(b):
                for c in range(C):
                    r = v.tensor_copy(cr[:, c], cx[:, c, b, None, :].broadcast_to([P, HG, KP]))
                r.then_inc(s["cr_done"], 1)

            def value_lo(n):
                b, m = n // M, n % M
                dve.wait_ge(s["vp"], n + 1)
                vt = xres[0:MK, n % 2, :].rearrange("p (j n) -> p j n", j=J)
                for j in range(J):
                    r = v.tensor_tensor(vt[:, j].rearrange("p (h n) -> p h n", h=HG),
                                        bP[n % 2][0:MK, j * P:(j + 1) * P].rearrange("p (h n) -> p h n", h=HG),
                                        hsel[0:MK, m, :, None].broadcast_to([MK, HG, HD]), ALU.mult)
                r.then_inc(s["v_tmp"], 1)
                v.tensor_copy(vbd[0:MK, b, :, m, P:VC],
                              hsel[0:MK, m, None, :].broadcast_to([MK, J, HG]))
                dve.wait_ge(s["v_hi"], n + 1)
                lo(vbd[0:MK, b, :, m, VC:VW], vt, vbd[0:MK, b, :, m, 0:P]).then_inc(s["v_lo"], 1)

            dve.wait_ge(s["ld_ctx"], 16 * B)
            repeat_rows(0)
            for j in range(J):
                ktmp = ktmps[j % 2]
                for h in range(HG):
                    rs = slice(h * HD, (h + 1) * HD)
                    dve.wait_ge(s["k_hi"], HG * j + h + 1)
                    lo(kbd[rs, 1, :, j, h * KP:h * KP + KEYS], ktmp[rs],
                       kbd[rs, 0, :, j, h * KP:h * KP + KEYS]).then_inc(s["k_lo"], 1)
            dve.wait_ge(s["const_tiles"], 7)
            dve.wait_ge(s["ld_mask"], 16)
            v.tensor_scalar(mbias[:, :, :], mraw[:, :, :], MASKED, None, ALU.mult)

            def pl(t, j):
                dve.wait_ge(s["ph"], 4 * t + j + 1)
                lo(pT[0:MK, j % 2, 1, :], bP[j % 2][0:MK, 0:M * P], pT[0:MK, j % 2, 0, :]).then_inc(s["pl"], 1)

            def mask_add(t, j):
                dve.wait_ge(s["sp"], 4 * t + j + 1)
                if t >= 2 and j == 0:
                    dve.wait_ge(s["pt"], 4 * (t - 1))
                if t == 0 and j == 0:
                    dve.wait_ge(s["wo_lo"], 1)
                    dve.wait_ge(s["kp"], J)
                g, i = t // GT, t % GT
                mt = 2 * g + i % 2
                v.tensor_tensor(smx[:, t % 2, j * GK:(j + 1) * GK].rearrange("p (h n) -> p h n", h=HG),
                                bS[j % 2][:, 0:GK].rearrange("p (h n) -> p h n", h=HG),
                                mbias[:, bass.ds(mt, 1), :].broadcast_to([P, HG, KP]), ALU.add).then_inc(s["ma"], 1)

            def context_sum(t, j):
                bank = bV if j % 2 == 0 else bQ
                dve.wait_ge(s["c_lo"], 4 * t + j + 1)
                v.reciprocal(rden[:, j, :], bank[:, P:VC]).then_inc(s["rc"], 1)
                c = ctok[:, t % 2, j * P:(j + 1) * P]
                v.tensor_tensor(c, bank[:, 0:P], c, ALU.add).then_inc(s["csum"], 1)

            def context_T_lo(t):
                dve.wait_ge(s["ch"], t + 1)
                lo(cT[:, 1, :], bT[:, :], cT[:, 0, :]).then_inc(s["cl"], 1)

            def context(t):
                dve.wait_ge(s["csum"], 4 * t + 4)
                dve.wait_ge(s["rc"], 4 * t + 4)
                c = ctok[:, t % 2, :].rearrange("p (g n) -> p g n", n=HD)
                v.tensor_tensor(c, c, rden[:, :, :].rearrange("p j h -> p (j h)")[:, :, None].broadcast_to(
                    [P, HEADS, HD]), ALU.mult).then_inc(s["cn"], 1)

            def split_lo(e, ch):
                dve.wait_ge(s["whi"], e * WCH + ch + 1)
                w = e % 2

                def at_(h):
                    return (w_gu[w][h][:, ch, :] if ch < 4 else
                            w_dn[w][h][:, 2 * (ch - 4):2 * (ch - 4) + 2, :].rearrange("p c n -> p (c n)"))
                lo(at_(1), wraw[:, w_slot(e, ch), :], at_(0)).then_inc(s["wlo"], 1)

            def route_choice(g):
                n = ROUTE_STEPS * g
                dve.wait_ge(s["lgd"], GT * (g + 1))
                for i in range(GT):
                    v.max(top[:, i, :], lg[:, g % 2, i, :]).then_inc(s["route"], 1)
                dve.wait_ge(s["route"], n + GT)
                for i in range(GT):
                    v.max_index(topi[:, i, :], top[:, i, :], lg[:, g % 2, i, :]).then_inc(s["route"], 1)
                v.tensor_tensor(dif[:, :, :], top[:, :, :], top[:, :, 0:1].broadcast_to([P, GT, E]),
                                ALU.subtract).then_inc(s["dif_d"], 1)
                dve.wait_ge(s["route"], n + 2 * GT)
                v.tensor_copy(topf[:, :, :], topi[:, :, 0:2]).then_inc(s["route"], 1)
                dve.wait_ge(s["route"], n + 2 * GT + 1)
                for k in range(2):
                    v.tensor_tensor(hot[:, k], iota8[:, None, :].broadcast_to([P, GT, E]),
                                    topf[:, :, k:k + 1].broadcast_to([P, GT, E]), ALU.is_equal).then_inc(s["route"], 1)
                dve.wait_ge(s["route"], n + 2 * GT + 3)
                v.tensor_tensor(picked[:, 0:GT, :], hot[:, 0], hot[:, 1], ALU.add).then_inc(s["hot_d"], 1)

            def normalise(n):
                dve.wait_ge(s["route"], n)
                v.scalar_tensor_tensor(zs[:, :, 0], pp[:, :, 0], TOPK_EPS, pp[:, :, 1], ALU.add, ALU.add).then_inc(s["route"], 1)
                dve.wait_ge(s["route"], n + 1)
                v.reciprocal(rz[:, :, 0], zs[:, :, 0]).then_inc(s["route"], 1)
                dve.wait_ge(s["route"], n + 2)
                v.tensor_tensor(pp[:, :, :], pp[:, :, :], rz[:, :, :].broadcast_to([P, GT, 2]), ALU.mult).then_inc(s["route"], 1)

            def route_softmax(g):
                n = ROUTE_STEPS * g + 2 * GT + 3
                dve.wait_ge(s["exr"], g + 1)
                v.tensor_reduce(zs[:, :, 0], ex[:, :, :], AX.X, ALU.add).then_inc(s["route"], 1)
                dve.wait_ge(s["route"], n + 1)
                v.reciprocal(rz[:, :, 0], zs[:, :, 0]).then_inc(s["route"], 1)
                dve.wait_ge(s["route"], n + 2)
                v.tensor_tensor(pp[:, :, :], ex[:, :, 0:2], rz[:, :, :].broadcast_to([P, GT, 2]), ALU.mult).then_inc(s["route"], 1)
                normalise(n + 3)

            def route_weights(g):
                n = ROUTE_STEPS * g + 2 * GT + 3
                q = g % 2
                normalise(n + 6)
                dve.wait_ge(s["route"], n + 9)
                for k in range(2):
                    v.tensor_tensor(tmp[:, k], hot[:, k], pp[:, :, k:k + 1].broadcast_to([P, GT, E]), ALU.mult).then_inc(s["route"], 1)
                v.tensor_copy(rows[:, q, :, D].bitcast(U32), toki[:, bass.ds(g * GT, GT)]).then_inc(s["route"], 1)
                dve.wait_ge(s["route"], n + 11)
                v.tensor_tensor(rows[:, q, :, D + 1:ROW], tmp[:, 0], tmp[:, 1], ALU.add).then_inc(s["route"], 1)

            def route_slots(g):
                n = ROUTE_STEPS * g + 2 * GT + 16
                dve.wait_ge(s["rank_d"], g + 1)
                v.tensor_tensor(slot[:, :, :], rank[:, 0:GT, :],
                                count[:, None, :].broadcast_to([P, GT, E]), ALU.add).then_inc(s["hot_d"], 1)
                dve.wait_ge(s["hot_d"], 3 * g + 2)
                v.tensor_tensor(count[:, :], count[:, :], rank[:, GT, :], ALU.add).then_inc(s["hot_d"], 1)
                dve.wait_ge(s["route"], n)
                for k in range(2):
                    v.tensor_tensor(tmp[:, k], slot[:, :, :], hot[:, k], ALU.mult).then_inc(s["route"], 1)
                dve.wait_ge(s["route"], n + 2)
                v.tensor_reduce(slotf[:, :, :], tmp[:, :, :, :], AX.X, ALU.add).then_inc(s["route"], 1)
                dve.wait_ge(s["route"], n + 3)
                v.tensor_copy(sloti[:, g % 2, :, :], slotf[:, :, :]).then_inc(s["route"], 1)

            for st in STEPS:
                g, i = st // GT, st % GT
                if st == V_STEP + M - 1:
                    dve.wait_ge(s["vp"], M)
                    repeat_rows(1)
                if st < 0:
                    ln_x(st + 9)
                if has(st - 2) and st >= W0_STEP:
                    context(st - 2)
                if has(st):
                    mask_add(st, 0)
                    mask_add(st, 1)
                if has(st - 1):
                    pl(st - 1, 0)
                if has(st + 8):
                    t = st + 8
                    dve.wait_ge(s["xh"], t + 1)
                    cs = slice((t % GT) * P, (t % GT + 1) * P)
                    lo(xT[(t // GT) % 2][:, 1, :, cs], bT[:, :].rearrange("p (c n) -> p c n", c=C),
                       xT[(t // GT) % 2][:, 0, :, cs]).then_inc(s["xl"], 1)
                if has(st):
                    mask_add(st, 2)
                if has(st - 1):
                    pl(st - 1, 1)
                if has(st):
                    mask_add(st, 3)
                if has(st - 2) and st < W0_STEP:
                    context(st - 2)
                if has(st - 2) and st >= W0_STEP:
                    context_T_lo(st - 2)
                if has(st):
                    dve.wait_ge(s["ma"], 4 * st + 4)
                    v.tensor_reduce(mxs[:, st % 2, :], smx[:, st % 2, :].rearrange("p (h n) -> p h n", h=HEADS),
                                    AX.X, ALU.max).then_inc(s["mxd"], 1)
                gq = g + 1
                if 0 <= gq < GROUPS:
                    dve.wait_ge(s["qh"], 4 * gq + i + 1)
                    v.scalar_tensor_tensor(qT[gq % 2][:, 1, i, :], bQ[:, :], qb_s[:, i:i + 1], f(qT[gq % 2][:, 0, i, :]),
                                           ALU.add, ALU.subtract).then_inc(s["ql"], 1)
                if st == WQ_STEP:
                    dve.wait_ge(s["wq_hi"], 1)
                    lo(wq_s[:, 1].rearrange("p c n -> p (c n)"), stage[:, 4 * D:8 * D],
                       wq_s[:, 0].rearrange("p c n -> p (c n)")).then_inc(s["wq_lo"], 1)
                if st == -1:
                    dve.wait_ge(s["wo_hi"], 1)
                    lo(wo_s[:, 1].rearrange("p c n -> p (c n)"), stage[:, 4 * D:8 * D],
                       wo_s[:, 0].rearrange("p c n -> p (c n)")).then_inc(s["wo_lo"], 1)
                if 0 <= st - V_STEP < B * M:
                    value_lo(st - V_STEP)
                if has(st - 2) and st < W0_STEP:
                    context_T_lo(st - 2)
                if st >= 0 and has(st + 9):
                    ln_x(st + 9)
                if has(st - 1):
                    context_sum(st - 1, 0)
                    context_sum(st - 1, 1)
                    pl(st - 1, 2)
                    pl(st - 1, 3)
                if 0 < st - W0_STEP <= WCH:
                    split_lo(0, st - W0_STEP - 1)
                if (st - 7) % GT == 0 and has(st - 7):
                    route_choice((st - 7) // GT)
                if (st - 8) % GT == 0 and has(st - 8):
                    route_softmax((st - 8) // GT)
                if (st - 9) % GT == 0 and has(st - 9):
                    route_weights((st - 9) // GT)
                if (st - 10) % GT == 0 and has(st - 10):
                    route_slots((st - 10) // GT)
                if has(st - 2):
                    t = st - 2
                    dve.wait_ge(s["op"], t + 1)
                    dve.wait_ge(s["xb"], t + 1)
                    if t >= 2:
                        dve.wait_ge(x_st[t % 2], 16 * (t // 2))
                        dve.wait_ge(s["hn"], t - 1)
                    v.tensor_tensor(x2[:, t % 2, :], bO[:, :], xres[:, t % 2, :], ALU.add).then_inc(s["x2d"], 1)
                    dve.wait_ge(s["x2d"], t + 1)
                    ln(t, x2[:, t % 2, :], st2, mv2, ve2, "ln2")
                if has(st - 1):
                    context_sum(st - 1, 2)
                    context_sum(st - 1, 3)
                if has(st - 3):
                    t = st - 3
                    dve.wait_ge(s["rt"], t + 1)
                    if (st - 7) % GT == 0 and has(st - 7):
                        dve.wait_ge(s["rank"], (st - 7) // GT + 1)
                    v.tensor_copy(lg[:, (t // GT) % 2, t % GT, :], LOGITS).then_inc(s["lgd"], 1)
                if (st - 7) % GT == 0 and has(st - 7):
                    dve.wait_ge(s["rank"], (st - 7) // GT + 1)
                    v.tensor_copy(rank[:, :, :], RANK).then_inc(s["rank_d"], 1)

            dve.wait_ge(s["hot_d"], 3 * GROUPS)
            v.tensor_tensor(ntok[:, :], count[:, :], first[:, :], ALU.subtract).then_inc(s["cchain"], 1)
            dve.wait_ge(s["cchain"], 1)
            v.tensor_scalar(ntile[:, :], ntok[:, :], float(P - 1), None, ALU.add).then_inc(s["cchain"], 1)
            dve.wait_ge(s["cchain"], 2)
            v.tensor_scalar(ntile[:, :], ntile[:, :], 7, None, ALU.logical_shift_right).then_inc(s["cchain"], 1)
            dve.wait_ge(s["cchain"], 3)
            v.tensor_scalar(ntile[:, :], ntile[:, :], float(MINT), None, ALU.max).then_inc(s["cchain"], 1)
            v.memset(tbase[:, 0:1], -1).then_inc(s["cchain"], 1)
            for e in range(E):
                dve.wait_ge(s["cchain"], 5 + e)
                v.tensor_tensor(tbase[:, e + 1:e + 2], tbase[:, e:e + 1], ntile[:, e:e + 1], ALU.add).then_inc(s["cchain"], 1)
            dve.wait_ge(s["cchain"], 5 + E)
            v.memset(zs[:, :, :], 0.0).then_inc(s["counts"], 1)

            def rows_lo(p):
                dve.wait_ge(s["rxh"], p + 3)
                lo(rT[:, 1, :], bQ[:, :], rT[:, 0, :]).then_inc(s["rxl"], 1)
                if not isinstance(p, int) or p > -1:
                    dve.wait_ge(s["mshift"], 2 * p + 2)
                elif p == -1:
                    dve.wait_ge(s["zrow"], 2)
                v.tensor_copy(meta[0][:, :], rowb[:, D:ROW].bitcast(U32)).then_inc(s["m0"], 1)

            def hidden_lo(p):
                dve.wait_ge(s["hh"], p + 1)
                lo(hT[:, 1, :], bT[:, :], hT[:, 0, :]).then_inc(s["hl"], 1)

            def hidden(t):
                dve.wait_ge(s["sgd"], t + 1)
                dve.wait_ge(s["up"], t + 1)
                if not isinstance(t, int) or t > 0:
                    dve.wait_ge(s["th2"], t)
                v.tensor_tensor(hid, bS1[:, :], sg, ALU.mult).then_inc(s["hm"], 1)

            def accumulate(e, p):
                dve.wait_ge(s["dnp"], p + 1)
                dve.wait_ge(s["mshift"], 2 * p + 2)
                if not isinstance(p, int) or p > 0:
                    dve.wait_ge(s["sct"], 16 * p)
                v.tensor_scalar(acc, bO[:, :], meta[2][:, 1 + e:2 + e].bitcast(F32), None, ALU.mult).then_inc(s["accd"], 1)

            rows_lo(-2)
            for e in range(E):
                cnt = dve.value_load(ntile[0:1, e:e + 1], min_val=MINT, max_val=B * S // P)
                before = dve.value_load(tbase[0:1, e:e + 1], min_val=0, max_val=MAXT) if e else -1
                for k in range(2):
                    p = before + k
                    if e or k:
                        hidden_lo(p)
                    if e + 1 < E:
                        split_lo(e + 1, 3 * k)
                    hidden(p + 1)
                    rows_lo(p)
                    if e + 1 < E:
                        split_lo(e + 1, 3 * k + 1)
                    if e or k:
                        accumulate(e if k else e - 1, p)
                    if e + 1 < E:
                        split_lo(e + 1, 3 * k + 2)
                with dve.Fori(1, cnt - 1) as k:
                    p = before + 1 + k
                    hidden_lo(p)
                    hidden(p + 1)
                    rows_lo(p)
                    accumulate(e, p)
            last = dve.value_load(tbase[0:1, E:E + 1], min_val=0, max_val=MAXT)
            hidden_lo(last)
            accumulate(E - 1, last)

        @block.tensor
        def _(pe):
            te = nc.tensor

            def three(o, ws, xs, n):
                for c in range(n):
                    for at, (a, b) in enumerate(((0, 0), (0, 1), (1, 0))):
                        r = te.matmul(o, ws(a, c), xs(b, c), start=(c == 0 and at == 0),
                                      stop=(c == n - 1 and at == 2))
                return r

            def transposes(bank, src):
                for c in range(C):
                    r = te.transpose(bank[:, c * P:(c + 1) * P], src[:, c * P:(c + 1) * P], ident[:, :])
                return r

            cx = rflat[:, 4 * D:4 * D + C * B * KP].rearrange("p (c b n) -> p c b n", c=C, b=B)
            cr = rflat[:, 4 * D + C * B * KP:4 * D + C * B * KP + C * GK].rearrange("p (c n) -> p c n", c=C)
            wk_r = stage[:, 8 * D:12 * D].rearrange("p (c n) -> p c n", c=C)
            wv_r = rflat[:, 0:4 * D].rearrange("p (c n) -> p c n", c=C)
            pe.wait_ge(s["ld_wk"], 16)
            pe.wait_ge(s["ld_ctx"], 16 * B)
            for j in range(J):
                if j >= 2:
                    pe.wait_ge(s["kp_out"], j - 1)
                for c in range(C):
                    r = te.matmul(bP[j % 2][:, 0:B * KEYS].rearrange("p (b n) -> p b n", b=B),
                                  wk_r[:, c, j * P:(j + 1) * P], cx[:, c, :, 0:KEYS], start=(c == 0), stop=(c == C - 1))
                r.then_inc(s["kp"], 1)
            def value_product(n):
                b, m = n // M, n % M
                if n == 0:
                    pe.wait_ge(s["const_tiles"], 7)
                    pe.wait_ge(s["ld_wv"], 16)
                    pe.wait_ge(s["ld_small"], 16 * 4)
                    pe.wait_ge(s["kp_out"], J)
                pe.wait_ge(s["cr_done"], b + 1)
                if n >= 2:
                    pe.wait_ge(s["v_tmp"], n - 1)
                te.matmul(bP[n % 2][0:MK, :], ones1[0:1, 0:MK], vb_s[0:1, :], start=True, stop=False)
                for c in range(C):
                    r = te.matmul(bP[n % 2][0:MK, :], cr[:, c, m * MK:(m + 1) * MK], wv_r[:, c, :],
                                  start=False, stop=(c == C - 1))
                r.then_inc(s["vp"], 1)

            def scores(t, j):
                g, b = t // GT, (t % GT) // 2
                if t % GT == 0 and j == 0:
                    pe.wait_ge(s["ql"], 4 * (g + 1))
                if t == 0 and j == 0:
                    pe.wait_ge(s["k_lo"], J * HG)
                n = 4 * t + j
                if n >= 2:
                    pe.wait_ge(s["ma"], n - 1)
                cs = slice((t % GT) * P, (t % GT + 1) * P)
                q = qT[g % 2]
                three(bS[j % 2][:, 0:GK], lambda h, c: q[:, h, j, cs], lambda h, c: kbd[:, h, b, j, :], 1).then_inc(s["sp"], 1)

            def probs_T(t, j):
                n = 4 * t + j
                if j == 0:
                    pe.wait_ge(s["ex_done"], t + 1)
                if n >= 2:
                    pe.wait_ge(s["pl"], n - 1)
                elif n == 0:
                    pe.wait_ge(s["v_tmp"], B * M)
                for m in range(M):
                    at = j * GK + m * MK
                    r = te.transpose(bP[j % 2][0:MK, m * P:(m + 1) * P], smx[:, t % 2, at:at + MK], ident[:, :])
                r.then_inc(s["pt"], 1)

            def values(t, j):
                b = (t % GT) // 2
                bank = bV if j % 2 == 0 else bQ
                pe.wait_ge(s["pl"], 4 * t + j + 1)
                if 4 * t + j > 1:
                    pe.wait_ge(s["csum"], 4 * t + j - 1)
                if j == 1 and t + 1 + GT < TILES:
                    pe.wait_ge(s["ql"], t + 2 + GT)
                if t == 0 and j == 0:
                    pe.wait_ge(s["v_lo"], B * M)

                def prod(h, m, start=False, stop=False):
                    n = VC if h else VW
                    return te.matmul(bank[:, 0:n], pT[0:MK, j % 2, h, m * P:(m + 1) * P],
                                     vbd[0:MK, b, j, m, 0:n], start=start, stop=stop)

                prod(0, 0, start=True)
                for m in range(M):
                    prod(1, m)
                for m in range(1, M):
                    r = prod(0, m, stop=(m == M - 1))
                r.then_inc(s["pv"], 1)

            for st in STEPS:
                g, i = st // GT, st % GT
                if has(st):
                    scores(st, 0)
                    scores(st, 1)
                if has(st - 1):
                    probs_T(st - 1, 0)
                if 0 <= st - V_STEP < B * M:
                    value_product(st - V_STEP)
                if has(st + 8):
                    t = st + 8
                    pe.wait_ge(s["xn"], t + 1)
                    if t >= 1:
                        pe.wait_ge(s["xl"], t)
                    transposes(bT, xin[:, t % 4, :]).then_inc(s["tx"], 1)
                if has(st):
                    scores(st, 2)
                if has(st - 1):
                    probs_T(st - 1, 1)
                if has(st):
                    scores(st, 3)
                gq = g + 1
                if 0 <= gq < GROUPS:
                    if i == 0:
                        pe.wait_ge(s["xl"], 4 * gq + 4)
                    if gq == 0 and i == 0:
                        pe.wait_ge(s["wq_lo"], 1)
                    if gq or i:
                        pe.wait_ge(s["ql"], 4 * gq + i)
                    if st >= 2:
                        pe.wait_ge(s["csum"], 4 * (st - 1))
                    xx = xT[gq % 2]
                    three(bQ[:, :], lambda h, c: wq_s[:, h, c, i * P:(i + 1) * P], lambda h, c: xx[:, h, c, :], C).then_inc(s["qp"], 1)
                if has(st - 2):
                    t = st - 2
                    pe.wait_ge(s["cn"], t + 1)
                    pe.wait_ge(s["xl"], min(TILES, st + 9))
                    transposes(bT, ctok[:, t % 2, :]).then_inc(s["tc"], 1)
                if has(st - 1):
                    values(st - 1, 0)
                    probs_T(st - 1, 2)
                    probs_T(st - 1, 3)
                    values(st - 1, 1)
                if has(st - 3):
                    t = st - 3
                    pe.wait_ge(s["hn"], t + 1)
                    pe.wait_ge(s["cl"], min(TILES, st - 1))
                    transposes(bT, rows[:, (t // GT) % 2, t % GT, 0:D]).then_inc(s["th"], 1)
                if has(st - 2):
                    t = st - 2
                    pe.wait_ge(s["cl"], t + 1)
                    if t >= 1:
                        pe.wait_ge(s["x2d"], t)
                    if t >= 2:
                        pe.wait_ge(s["lgd"], t - 1)
                    if (st - 8) % GT == 0 and has(st - 8):
                        pe.wait_ge(s["rank_d"], (st - 8) // GT + 1)
                    if t == 0:
                        pe.wait_ge(s["wo_lo"], 1)
                    three(bO[:, :], lambda h, c: cT[:, h, c * P:(c + 1) * P], lambda h, c: wo_s[:, h, c, :], C).then_inc(s["op"], 1)
                if has(st - 1):
                    values(st - 1, 2)
                    values(st - 1, 3)
                if has(st - 3):
                    t = st - 3
                    pe.wait_ge(s["h2"], t + 1)
                    pe.wait_ge(s["x2d"], min(TILES, st - 1))
                    if t >= 1:
                        pe.wait_ge(s["lgd"], t)
                    for c in range(C):
                        r = te.matmul(LOGITS, h2T[:, c * P:(c + 1) * P], gw_s[:, c, :], start=(c == 0), stop=(c == C - 1))
                    r.then_inc(s["rt"], 1)
                gr = (st - 7) // GT
                if (st - 7) % GT == 0 and 0 <= gr < GROUPS:
                    pe.wait_ge(s["hot_d"], 3 * gr + 1)
                    pe.wait_ge(s["lgd"], st - 3)
                    te.matmul(RANK, tri[:, :], picked[:, :, :], start=True, stop=False)
                    for j in range(GT):
                        r = te.matmul(RANK[:, j + 1:GT + 1, :], ones[:, :],
                                      picked[:, j:j + 1, :].broadcast_to([P, GT - j, E]), start=False, stop=(j == GT - 1))
                    r.then_inc(s["rank"], 1)

            pe.wait_ge(s["counts"], 1)

            def rows_T(t):
                pe.wait_ge(s["rw"], 16 * t + 16)
                if not isinstance(t, int) or t > 0:
                    pe.wait_ge(s["rxl"], t)
                transposes(bQ, rowb[:, 0:D]).then_inc(s["tx2"], 1)

            def half(t, w, u):
                cs = slice(u * FF, (u + 1) * FF)
                return three(bS[u][:, :], lambda h, c: rT[:, h, c * P:(c + 1) * P], lambda h, c: w_gu[w][h][:, c, cs], C)

            def gates(t, w):
                pe.wait_ge(s["rxl"], t + 1)
                if not isinstance(t, int) or t > 0:
                    pe.wait_ge(s["sgd"], t)
                half(t, w, 0).then_inc(s["gt"], 1)

            def hidden_T(p):
                pe.wait_ge(s["hm"], p + 1)
                if not isinstance(p, int) or p > 0:
                    pe.wait_ge(s["hl"], p)
                transposes(bT, hid).then_inc(s["th2"], 1)

            def ups(t, w):
                half(t, w, 1).then_inc(s["up"], 1)

            def down(p, w):
                pe.wait_ge(s["hl"], p + 1)
                if not isinstance(p, int) or p > 0:
                    pe.wait_ge(s["accd"], p)
                three(bO[:, :], lambda h, c: hT[:, h, c * P:(c + 1) * P], lambda h, c: w_dn[w][h][:, c, :], C).then_inc(s["dnp"], 1)

            rows_T(0)
            for e in range(E):
                w = e % 2
                cnt = pe.value_load(ntile[0:1, e:e + 1], min_val=MINT, max_val=B * S // P)
                before = pe.value_load(tbase[0:1, e:e + 1], min_val=0, max_val=MAXT) if e else -1
                pe.wait_ge(s["wlo"], WCH * (e + 1))
                for k in range(2):
                    p = before + k
                    gates(p + 1, w)
                    if e or k:
                        hidden_T(p)
                    ups(p + 1, w)
                    rows_T(p + 2)
                    if e or k:
                        down(p, w if k else 1 - w)
                with pe.Fori(1, cnt - 1) as k:
                    p = before + 1 + k
                    gates(p + 1, w)
                    hidden_T(p)
                    ups(p + 1, w)
                    rows_T(p + 2)
                    down(p, w)
            last = pe.value_load(tbase[0:1, E:E + 1], min_val=0, max_val=MAXT)
            hidden_T(last)
            down(last, (E - 1) % 2)


_INS = ["x", "ctxT", "mask", "wq", "q_b", "wk", "k_b", "wv", "v_b", "wo", "o_b", "gw", "gu", "dn"]


def kernel(x, ctx_1024, mask_SxS2_bk1, L0_xattn_q_w, L0_xattn_q_b, L0_xattn_k_w, L0_xattn_k_b,
           L0_xattn_v_w, L0_xattn_v_b, L0_xattn_o_w, L0_xattn_o_b, L0_ffn_gate_w, L0_ffn_gate_up_proj,
           L0_ffn_down_proj):
    import numpy as np
    import concourse.bacc as bacc
    from concourse.bass_utils import run_bass_kernel_spmd

    def rows_first(a):
        a = np.asarray(a)
        return np.ascontiguousarray(a.reshape(-1, P, a.shape[1]).transpose(1, 0, 2))

    def by_head_group(b):
        return np.ascontiguousarray(np.asarray(b).reshape(J, P).T)

    def turned(w):
        return rows_first(np.asarray(w).T)

    given = {
        "x": x, "ctxT": np.stack([turned(c) for c in np.asarray(ctx_1024)]),
        "mask": rows_first(mask_SxS2_bk1),
        "wq": turned(L0_xattn_q_w), "q_b": by_head_group(L0_xattn_q_b),
        "wk": turned(L0_xattn_k_w), "k_b": by_head_group(L0_xattn_k_b),
        "wv": turned(L0_xattn_v_w), "v_b": L0_xattn_v_b, "wo": turned(L0_xattn_o_w), "o_b": L0_xattn_o_b,
        "gw": turned(L0_ffn_gate_w), "gu": L0_ffn_gate_up_proj, "dn": L0_ffn_down_proj,
    }
    nc = bacc.Bacc("TRN2", target_bir_lowering=False, num_devices=1)
    arrays, args = {}, []
    for name in _INS:
        a = np.ascontiguousarray(given[name])
        arrays[f"in_{name}"] = a
        args.append(nc.dram_tensor(f"in_{name}", a.shape, mybir.dt.from_np(a.dtype), kind="ExternalInput").ap())
    args.append(nc.dram_tensor("out_0", (B, S, D), F32, kind="ExternalOutput").ap())
    build(nc, *args)
    r = run_bass_kernel_spmd(nc, [arrays], core_ids=[0])
    return r.results[0]["out_0"]
```
